# Optimizing a Trainium2 kernel written in Bass

```python
import numpy as np
import jax
import jax.numpy as jnp

def _softmax(x, axis=-1):
    return jax.nn.softmax(x, axis=axis)

def _gelu(x):
    return jax.nn.gelu(x, approximate=True)

def _silu(x):
    return jax.nn.silu(x)

def _sigmoid(x):
    return jax.nn.sigmoid(x)

def _layernorm(x, axis=-1, eps=1e-05):
    m = jnp.mean(x, axis=axis, keepdims=True)
    v = jnp.var(x, axis=axis, keepdims=True)
    return (x - m) / jnp.sqrt(v + eps)

def _scatter_add(tgt, idx, src, axis=0):
    return tgt.at[idx].add(src)

def _segment_sum(src, seg, n):
    return jax.ops.segment_sum(src, seg, n)
kernel_name = 'mk_flamingo_gated_d1_seqx_r2_12b81b'

def setup_inputs(seed: int=0):
    np.random.seed(seed)
    _w = jnp.asarray

    def _rec_inputs():
        import jax
        import jax.numpy as jnp
        _rk = jax.random.key(seed)
        x = 4.136e-05 + 0.9999 * jax.random.normal(jax.random.fold_in(_rk, 1), (16, 512, 512), jnp.float32)
        _lenS = 512 - jax.random.randint(jax.random.fold_in(_rk, 7), (16,), 0, max(1, 512 // 4) + 1, jnp.int32)
        _lenS2 = 512 - jax.random.randint(jax.random.fold_in(_rk, 8), (16,), 0, max(1, 512 // 4) + 1, jnp.int32)
        _ctx_2048P = jax.random.normal(jax.random.fold_in(_rk, 11), (16, 16, 1024), jnp.float32)
        _ctx_2048c = jax.random.dirichlet(jax.random.fold_in(_rk, 511), 0.3 * jnp.ones((16,), jnp.float32), (16, 512))
        _ctx_2048t = jnp.einsum('bsk,bkd->bsd', _ctx_2048c, _ctx_2048P)
        _ctx_2048t = _ctx_2048t * jax.lax.rsqrt(jnp.mean(jnp.square(_ctx_2048t)) + 1e-12) * 0.953939
        ctx_2048 = -0.000392918 + 0.999932 * (_ctx_2048t + 0.3 * jax.random.normal(jax.random.fold_in(_rk, 611), (16, 512, 1024), jnp.float32))
        itok_Bx1_68_817 = jax.random.randint(jax.random.fold_in(_rk, 12), (16, 1), 68, 409, jnp.int32)
        _g = jax.random.normal(jax.random.fold_in(_rk, 9001), (2, 1), jnp.float32)
        _g = jnp.sign(_g) * jnp.maximum(jnp.abs(_g), 1.0) + (_g == 0) * 1.0
        g_xattn = _g[0]
        g_ffn = _g[1]
        return (x, ctx_2048, itok_Bx1_68_817, g_xattn, g_ffn)
    x, ctx_2048, itok_Bx1_68_817, g_xattn, g_ffn = _rec_inputs()

    def _L0_xattn_setup():
        import jax, jax.numpy as jnp
        import numpy as np
        UNITS = 512
        NUM_HEADS = 16
        MASK_VALUE = -1000000000000.0

        def _split_heads(x, n):
            B, S, D = x.shape
            return x.reshape(B, S, n, D // n).transpose(0, 2, 1, 3)
        key = jax.random.key(seed)
        k1, k2, k3, k4 = jax.random.split(key, 4)
        B, S = (8, 512)
        memory = jax.random.normal(k1, (B, S, 2 * UNITS), dtype=jnp.float32)
        query = jax.random.normal(k2, (B, S, UNITS), dtype=jnp.float32)
        b = jax.random.normal(k3, (S,), dtype=jnp.float32)
        seq_len = jax.random.randint(k4, (B, 1), 0, S, dtype=jnp.int32)
        return {'memory': memory, 'query': query, 'b': b, 'seq_len': seq_len}
    _L0_xattn_all = _L0_xattn_setup()
    _L0_xattn_in = {k: v for k, v in _L0_xattn_all.items() if k in ('b',)}
    del _L0_xattn_all

    def _L0_ffn_setup():
        import jax, jax.numpy as jnp
        import numpy as np
        D_MODEL = 512
        D_FF = 2048
        N_EXPERTS = 8
        D_EXPERT = D_FF // N_EXPERTS
        TOP_K = 2
        LB_WEIGHT = 0.01
        B, S = (4, 1024)

        def _top_k_softmax(logits, k):
            vals, _ = jax.lax.top_k(logits, k)
            thresh = vals[..., -1:]
            masked = jnp.where(logits >= thresh, logits, -jnp.inf)
            return jax.nn.softmax(masked, axis=-1)
        key = jax.random.key(seed)
        ks = jax.random.split(key, 8)
        x = jax.random.normal(ks[0], (B, S, D_MODEL), dtype=jnp.float32)
        w1 = jax.random.normal(ks[1], (N_EXPERTS, D_MODEL, D_EXPERT), dtype=jnp.float32) * (1.0 / np.sqrt(D_MODEL))
        b1 = jnp.zeros((N_EXPERTS, D_EXPERT), dtype=jnp.float32)
        w2 = jax.random.normal(ks[2], (N_EXPERTS, D_EXPERT, D_MODEL), dtype=jnp.float32) * (1.0 / np.sqrt(D_EXPERT))
        b2 = jnp.zeros((N_EXPERTS, D_MODEL), dtype=jnp.float32)
        centroids = jax.random.normal(ks[3], (N_EXPERTS, D_MODEL), dtype=jnp.float32) * 0.02
        w_route = jax.random.normal(ks[4], (N_EXPERTS, D_MODEL), dtype=jnp.float32) * (1.0 / np.sqrt(D_MODEL))
        return {'x': x, 'w1': w1, 'b1': b1, 'w2': w2, 'b2': b2, 'centroids': centroids, 'w_route': w_route}
    _L0_ffn_all = _L0_ffn_setup()
    _L0_ffn_in = {k: v for k, v in _L0_ffn_all.items() if k in ('w1', 'b1', 'w2', 'b2', 'centroids', 'w_route')}
    del _L0_ffn_all
    return {'x': x, 'ctx_2048': ctx_2048, 'itok_Bx1_68_817': itok_Bx1_68_817, 'g_xattn': g_xattn, 'g_ffn': g_ffn, 'L0_xattn_b': _L0_xattn_in['b'], 'L0_ffn_w1': _L0_ffn_in['w1'], 'L0_ffn_b1': _L0_ffn_in['b1'], 'L0_ffn_w2': _L0_ffn_in['w2'], 'L0_ffn_b2': _L0_ffn_in['b2'], 'L0_ffn_centroids': _L0_ffn_in['centroids'], 'L0_ffn_w_route': _L0_ffn_in['w_route']}

def reference(x, ctx_2048, itok_Bx1_68_817, g_xattn, g_ffn, L0_xattn_b, L0_ffn_w1, L0_ffn_b1, L0_ffn_w2, L0_ffn_b2, L0_ffn_centroids, L0_ffn_w_route):
    import jax
    import jax.numpy as jnp

    def _L0_xattn_ref(memory, query, b, seq_len):
        import jax, jax.numpy as jnp
        import numpy as np
        UNITS = 512
        NUM_HEADS = 16
        MASK_VALUE = -1000000000000.0

        def _split_heads(x, n):
            B, S, D = x.shape
            return x.reshape(B, S, n, D // n).transpose(0, 2, 1, 3)
        B, S, _ = query.shape
        dh = UNITS // NUM_HEADS
        k_mem, v_mem = jnp.split(memory, 2, axis=2)
        Q = _split_heads(query, NUM_HEADS) * dh ** (-0.5)
        Kh = _split_heads(k_mem, NUM_HEADS)
        Vh = _split_heads(v_mem, NUM_HEADS)
        logits = jnp.einsum('bhqd,bhkd->bhqk', Q, Kh) + b
        valid = (jnp.arange(S)[None, :] < seq_len[:, 0:1]).astype(jnp.float32)
        logits = logits + MASK_VALUE * (1.0 - valid)[:, None, None, :]
        weights = jax.nn.softmax(logits, axis=-1)
        out = jnp.einsum('bhqk,bhkd->bhqd', weights, Vh)
        return out.transpose(0, 2, 1, 3).reshape(B, S, UNITS)

    def _L0_ffn_ref(x, w1, b1, w2, b2, centroids, w_route):
        import jax, jax.numpy as jnp
        import numpy as np
        D_MODEL = 512
        D_FF = 2048
        N_EXPERTS = 8
        D_EXPERT = D_FF // N_EXPERTS
        TOP_K = 2
        LB_WEIGHT = 0.01
        B, S = (4, 1024)

        def _top_k_softmax(logits, k):
            vals, _ = jax.lax.top_k(logits, k)
            thresh = vals[..., -1:]
            masked = jnp.where(logits >= thresh, logits, -jnp.inf)
            return jax.nn.softmax(masked, axis=-1)
        eps = 1e-12
        x_norm = x / jnp.maximum(jnp.linalg.norm(x, axis=-1, keepdims=True), eps)
        c_norm = centroids / jnp.maximum(jnp.linalg.norm(centroids, axis=-1, keepdims=True), eps)
        cos_scores = jnp.einsum('bsd,ed->bse', x_norm, c_norm)
        route_scores = jnp.einsum('bsd,ed->bse', x, w_route)
        logits = cos_scores + route_scores
        gates = _top_k_softmax(logits, TOP_K)
        h = jax.nn.gelu(jnp.einsum('bsd,edh->bseh', x, w1) + b1, approximate=False)
        expert_out = jnp.einsum('bseh,ehd->bsed', h, w2) + b2
        out = jnp.einsum('bse,bsed->bsd', gates, expert_out)
        return out
    x = x + jnp.tanh(g_xattn[0]) * _L0_xattn_ref(ctx_2048, _layernorm(x, axis=-1), L0_xattn_b, itok_Bx1_68_817)
    x = x + jnp.tanh(g_ffn[0]) * _L0_ffn_ref(_layernorm(x, axis=-1), L0_ffn_w1, L0_ffn_b1, L0_ffn_w2, L0_ffn_b2, L0_ffn_centroids, L0_ffn_w_route)
    return x

_drawn_inputs = setup_inputs


def setup_inputs(seed=0):
    import zlib

    import numpy as np

    out = dict(_drawn_inputs(seed))
    spreads = {'L0_ffn_b1': (0.0, 0.1), 'L0_ffn_b2': (0.0, 0.1)}
    factors = {}
    for name, (base, spread) in spreads.items():
        noise = np.random.default_rng([zlib.crc32(name.encode()), seed]).standard_normal(out[name].shape)
        drawn = base * np.exp(spread * noise) if base else spread * noise
        out[name] = jnp.asarray(drawn.astype(out[name].dtype))
    for name, factor in factors.items():
        out[name] = (out[name] * factor).astype(out[name].dtype)
    return out
```

```python
from contextlib import ExitStack

import concourse.bass as bass
from concourse import mybir

F32 = mybir.dt.float32
F32R = mybir.dt.float32r
I32 = mybir.dt.int32
ALU = mybir.AluOpType
ACT = mybir.ActivationFunctionType
AX = mybir.AxisListType

P = 128
HG = 4
STEPS_IN_BODY = 8
LN_EPS = 1e-5
NORM_EPS = 1e-12
MASK = -1e12
ROUND = float(3 << 22)
RSQRT_BITS = float(0x5F3759DF)
FAR = float(1 << 20)


class Step:

    def __init__(self, rnd, l, groups):
        self.rnd, self.l, self.groups = rnd, l, groups

    def on(self, off):
        return self.rnd is not None or 0 <= self.l + off < self.groups

    def count(self, per, off, k):
        v = per * (self.l + off) + k
        return v if self.rnd is None else self.rnd * (per * STEPS_IN_BODY) + v

    def batch(self, per, off, k):
        v = per * ((self.l + off) // 4) + k
        return v if self.rnd is None else self.rnd * (per * STEPS_IN_BODY // 4) + v

    def pair(self, per, off, k):
        v = per * ((self.l + off) // 2) + k
        return v if self.rnd is None else self.rnd * (per * STEPS_IN_BODY // 2) + v

    def bpair(self, per, off, k):
        v = per * ((self.l + off) // 8) + k
        return v if self.rnd is None else self.rnd * (per * STEPS_IN_BODY // 8) + v

    def g(self, off=0):
        return (self.l + off) % 4


TURNS = [("T0", 3), ("XT", -5), ("T1", 3), ("MT", 1), ("T2", 3), ("RK", -6), ("DT", -1), ("T3", 3), ("OT", -1),
         ("T4", 3), ("LG", -5), ("T5", 3), ("T6", 3), ("T7", 3)]
FIRST, LAST = -8, 7


RSQRT_STEPS = 13


def rsqrt(dve, y, t, v, done, at, first=0, last=RSQRT_STEPS):
    for k in range(first, last):
        if k == 0:
            dve.tensor_scalar(y.bitcast(I32), v.bitcast(I32), -0.5, RSQRT_BITS, ALU.mult, ALU.add).then_inc(done, 1)
            continue
        dve.wait_ge(done, at(k))
        if k % 4 == 1:
            dve.tensor_tensor(t, y, y, ALU.mult).then_inc(done, 1)
        elif k % 4 == 2:
            dve.tensor_tensor(t, t, v, ALU.mult).then_inc(done, 1)
        elif k % 4 == 3:
            dve.tensor_scalar(t, t, -0.5, 1.5, ALU.mult, ALU.add).then_inc(done, 1)
        else:
            dve.tensor_tensor(y, y, t, ALU.mult).then_inc(done, 1)


def turn_table(groups):
    table, k = {}, 0
    for n in range(FIRST, groups + LAST):
        for name, off in TURNS:
            if 0 <= n + off < groups:
                table[(n, name)] = k
                k += 1
    return table


def flamingo_kernel(nc, x, ctx_in, lens, g_xattn, g_ffn, b_in, w1, b1, w2, b2, cent, w_route, out):
    B, S, D = x.shape
    E, _, DE = w1.shape
    H = 16
    DH = D // H
    NG = H // HG
    NT = S // P
    G = B * NG
    TOK = B * S
    KD = D // P
    KE = DE // P
    CAP = TOK
    BLK = 512
    LIST = E * CAP
    assert NG == 4 and NT == 4 and S == 512 and D == 512 and B % 2 == 0 and E == 8 and DH == 32
    W3 = 3 * DH
    LN2 = RSQRT_STEPS + 7
    LN1 = RSQRT_STEPS + 10
    turns = turn_table(G)
    per_round = len(TURNS) * STEPS_IN_BODY

    x_d = x.rearrange("b (i p) d -> b p i d", p=P)
    c_d = ctx_in.rearrange("b (i p) d -> b p i d", p=P)
    out_d = out.rearrange("b (i p) d -> b p i d", p=P)
    out_rows = out.rearrange("b s d -> (b s) d")
    xn_d = nc.dram_tensor("xn_rows", (TOK, D), F32).ap()
    bm_d = nc.dram_tensor("bias_mask_rows", (B, 2, S), F32).ap()
    list_d = nc.dram_tensor("expert_lists", (LIST + BLK, 2), I32).ap()
    tab_d = nc.dram_tensor("block_table", (P, 2), I32).ap()

    outer = ExitStack()
    with outer:
        def keep(name, shape, dt=F32):
            return outer.enter_context(nc.sbuf_tensor(name, shape, dt))

        def sem(name):
            return outer.enter_context(nc.semaphore(name))

        ident = keep("ident", [P, P])
        ones = keep("ones", [P, P])
        lower = keep("lower", [P, P])
        msum = keep("msum", [P, E])
        tab = keep("tab", [1, 2 * P + 5], I32)

        hold = keep("hold", [P, 9])

        N_ROUNDS = 2 * P + 4

        with ExitStack() as ctx:
            def sb(name, shape, dt=F32):
                return ctx.enter_context(nc.sbuf_tensor(name, shape, dt))

            def ps(name, shape):
                return ctx.enter_context(nc.psum_tensor(name, shape, F32))

            stA = sb("stA", [P, 4, HG, S], F32R)
            stB = sb("stB", [P, 4, HG, S], F32R)
            rowQ = sb("rowQ", [P, 2, NT, HG, W3], F32R)
            rowK = sb("rowK", [P, 2, NT, HG, W3], F32R)
            xin = sb("xin", [P, 2, NT, D])
            kin = sb("kin", [P, 2, NT, D])
            vin = sb("vin", [P, 2, NT, D])
            xres = sb("xres", [P, 2, NT, D])
            prob = sb("prob", [P, 2, HG, S])
            xg = sb("xg", [P, 2, NT, P])
            attT = sb("attT", [P, 2, S])
            sumT = sb("sumT", [P, 2, S])
            rsum = sb("rsum", [P, NT, HG])
            scaled = sb("scaled", [P, NT, P])
            xn2 = sb("xn2", [P, 2, D])
            xT = sb("xT", [P, KD, P])
            st6 = sb("st6", [P, NT, 6])
            mv = sb("mv", [P, NT, 2])
            mean = sb("mean", [P, 2, NT])
            varx = sb("varx", [P, NT])
            varx2 = sb("varx2", [P, NT])
            rstd = sb("rstd", [P, 2, NT])
            mx = sb("mx", [P, NT, HG])
            nm = sb("nm", [P, NT, 2, HG], F32R)
            mT = sb("mT", [2 * HG, S], F32R)
            tanh_a = sb("tanh_a", [P, 1])
            tanh_f = sb("tanh_f", [P, 1])
            live = sb("live", [P, B])
            routeT = sb("routeT", [P, KD, 2 * E])
            st6b = sb("st6b", [P, 6])
            mvb = sb("mvb", [P, 2])
            rsb = sb("rsb", [P, 2])
            rst = sb("rst", [P, 2])
            varb = sb("varb", [P, 2])
            nrm = sb("nrm", [P, 2])
            lg = sb("lg", [P, 2 * E])
            logit = sb("logit", [P, E])
            top8 = sb("top8", [P, 8])
            mask = sb("mask", [P, 2, E])
            shifted = sb("shifted", [P, 2, E])
            expo = sb("expo", [P, 2, E])
            chosen = sb("chosen", [P, E])
            gsum = sb("gsum", [P, 2])
            e_off = sb("e_off", [P, E])
            token = sb("token", [P, 1])
            slot_f = sb("slot_f", [P, E])
            slot = sb("slot", [P, 2, E], I32)
            entry = sb("entry", [P, 2, E, 2], I32)
            eo_i = sb("eo_i", [P, E], I32)
            tok_i = sb("tok_i", [P, 1], I32)

            banks = [ps(f"bank{i}", [P, 512]) for i in range(8)]
            psS, psM, psT, psO, psD = banks[0:2], banks[2:4], banks[4:6], banks[6], banks[7]

            with (nc.sbuf_tensor("len_i", [P, B], I32) as len_i,
                  nc.sbuf_tensor("len_f", [P, B], F32) as len_f,
                  nc.sbuf_tensor("len_c", [B, 2], I32) as len_c,
                  nc.sbuf_tensor("len_cf", [B, 2], F32) as len_cf,
                  nc.sbuf_tensor("kpos", [B, S], I32) as kpos,
                  nc.sbuf_tensor("b_split", [B, 2, S], F32R) as b_split,
                  nc.sbuf_tensor("gates_in", [P, 2], F32) as gates_in,
                  nc.sbuf_tensor("cn", [E, 3], F32) as cn,
                  nc.sbuf_tensor("empty", [P, LIST // P, 2], I32) as empty):
                kpos_f = xres[0:B, 0, 0, :]
                b_row = xres[0:B, 0, 1, :]
                b_all = xres[0:B, 0, 2, :]
                cen = xres[0:E, 1, 0, :]
                cen2 = xres[0:E, 1, 1, :]
                wro = xres[0:E, 1, 2, :]
                s_load = sem("setup_loaded")
                s_pool = sem("setup_pool")
                s_dve = sem("setup_dve")
                s_act = sem("setup_act")
                s_pe = sem("setup_pe")
                s_put = sem("setup_stored")
                with nc.Block() as block:
                    @block.sync
                    def _(sp):
                        sp.dma_start(len_i[:, :], lens.rearrange("b a -> a b").to_broadcast([P, B])).then_inc(s_load, 16)
                        sp.dma_start(len_c[:, 0:1], lens).then_inc(s_load, 16)
                        sp.dma_start(b_row, b_in.rearrange("(a s) -> a s", a=1).to_broadcast([B, S])).then_inc(s_load, 16)
                        sp.dma_start(gates_in[:, 0:1], g_xattn.rearrange("(a s) -> a s", a=1).to_broadcast([P, 1])).then_inc(s_load, 16)
                        sp.dma_start(gates_in[:, 1:2], g_ffn.rearrange("(a s) -> a s", a=1).to_broadcast([P, 1])).then_inc(s_load, 16)
                        sp.dma_start(cen, cent).then_inc(s_load, 16)
                        sp.dma_start(wro, w_route).then_inc(s_load, 16)
                        sp.wait_ge(s_pool, 8)
                        sp.dma_start(list_d[0:LIST, :].rearrange("(p c) t -> p c t", p=P), empty[:, :, :]).then_inc(s_put, 16)
                        sp.dma_start(list_d[LIST:LIST + BLK, :].rearrange("(p c) t -> p c t", p=P),
                                     empty[:, 0:BLK // P, :]).then_inc(s_put, 16)
                        sp.wait_ge(s_dve, 12)
                        sp.dma_start(bm_d, b_split[:, :, :].bitcast(F32)).then_inc(s_put, 16)
                        sp.wait_ge(s_put, 48)

                    @block.gpsimd
                    def _(pool):
                        pool.memset(ident[:, :], 0.0).then_inc(s_pool, 1)
                        pool.memset(lower[:, :], 0.0).then_inc(s_pool, 1)
                        pool.memset(ones[:, :], 1.0).then_inc(s_pool, 1)
                        pool.memset(msum[:, :], 0.0).then_inc(s_pool, 1)
                        pool.iota(kpos[:, :], pattern=[[1, S]], base=0, channel_multiplier=0).then_inc(s_pool, 1)
                        pool.iota(eo_i[:, :], pattern=[[CAP, E]], base=-int(FAR), channel_multiplier=0).then_inc(s_pool, 1)
                        pool.iota(tok_i[:, :], pattern=[[0, 1]], base=0, channel_multiplier=1).then_inc(s_pool, 1)
                        pool.memset(empty[:, :, :], int(FAR)).then_inc(s_pool, 1)
                        pool.wait_ge(s_pool, 8)
                        pool.affine_select(out=ident[:, :], in_=ident[:, :], compare_op=ALU.not_equal, fill=1.0,
                                           base=0, pattern=[[-1, P]], channel_multiplier=1).then_inc(s_pool, 1)
                        pool.affine_select(out=lower[:, :], in_=lower[:, :], compare_op=ALU.is_ge, fill=1.0,
                                           base=0, pattern=[[-1, P]], channel_multiplier=1).then_inc(s_pool, 1)

                    @block.vector
                    def _(dve):
                        dve.memset(stA[96:P, :, :, :].bitcast(F32), 1.0)
                        dve.memset(stB[96:P, :, :, :].bitcast(F32), 1.0)
                        dve.wait_ge(s_load, 16 * 7)
                        dve.wait_ge(s_pool, 7)
                        dve.tensor_copy(len_f[:, :], len_i[:, :]).then_inc(s_dve, 1)
                        dve.tensor_copy(len_cf[:, 0:1], len_c[:, 0:1]).then_inc(s_dve, 1)
                        dve.tensor_copy(kpos_f, kpos[:, :]).then_inc(s_dve, 1)
                        dve.wait_ge(s_dve, 3)
                        dve.tensor_scalar(live[:, :], len_f[:, :], 1.0, None, ALU.is_ge).then_inc(s_dve, 1)
                        dve.tensor_scalar(len_cf[:, 1:2], len_cf[:, 0:1], 1.0, None, ALU.is_ge).then_inc(s_dve, 1)
                        dve.tensor_scalar(b_all, kpos_f, len_cf[:, 0:1], MASK, ALU.is_ge, ALU.mult).then_inc(s_dve, 1)
                        dve.tensor_tensor_reduce(cen2, cen, cen, 1.0, 0.0, ALU.mult, ALU.add,
                                                 cn[:, 0:1]).then_inc(s_dve, 1)
                        dve.wait_ge(s_dve, 7)
                        dve.tensor_tensor(kpos_f, b_all, b_row, ALU.add).then_inc(s_dve, 1)
                        dve.tensor_scalar(cn[:, 1:2], cn[:, 0:1], NORM_EPS * NORM_EPS, None, ALU.max).then_inc(s_dve, 1)
                        dve.wait_ge(s_dve, 9)
                        dve.tensor_scalar(b_all, kpos_f, len_cf[:, 1:2], None, ALU.mult).then_inc(s_dve, 1)
                        dve.wait_ge(s_dve, 10)
                        dve.tensor_copy(b_split[:, 0, :], b_all).then_inc(s_dve, 1)
                        dve.wait_ge(s_dve, 11)
                        dve.tensor_tensor(b_split[:, 1, :], b_all, b_split[:, 0, :].bitcast(F32),
                                          ALU.subtract).then_inc(s_dve, 1)
                        dve.tensor_copy(e_off[:, :], eo_i[:, :]).then_inc(s_dve, 1)
                        dve.tensor_copy(token[:, :], tok_i[:, :]).then_inc(s_dve, 1)
                        dve.wait_ge(s_dve, 14)
                        rsqrt(dve, cn[:, 0:1], cn[:, 2:3], cn[:, 1:2], s_dve, lambda k: 14 + k)
                        dve.wait_ge(s_dve, 14 + RSQRT_STEPS)
                        dve.tensor_scalar(cen2, cen, cn[:, 0:1], None, ALU.mult).then_inc(s_dve, 1)
                        dve.wait_ge(s_pe, 1)
                        dve.tensor_copy(routeT[:, :, :], psT[0][:, 0:KD * 2 * E].rearrange("p (k e) -> p k e", k=KD)).then_inc(s_dve, 1)

                    @block.scalar
                    def _(act):
                        act.wait_ge(s_load, 16 * 7)
                        act.activation(tanh_a[:, :], gates_in[:, 0:1], ACT.Tanh).then_inc(s_act, 1)
                        act.activation(tanh_f[:, :], gates_in[:, 1:2], ACT.Tanh).then_inc(s_act, 1)

                    @block.tensor
                    def _(pe):
                        pe.wait_ge(s_load, 16 * 7)
                        pe.wait_ge(s_pool, 10)
                        pe.wait_ge(s_dve, 15 + RSQRT_STEPS)
                        for k in range(KD):
                            pe.transpose(psT[0][:, 2 * E * k:2 * E * k + E], cen2[:, k * P:(k + 1) * P], ident[0:E, 0:E])
                            last = pe.transpose(psT[0][:, 2 * E * k + E:2 * E * k + 2 * E], wro[:, k * P:(k + 1) * P],
                                                ident[0:E, 0:E])
                        last.then_inc(s_pe, 1)

            s_x = [sem(f"x_loaded{i}") for i in range(2)]
            s_k = [sem(f"k_loaded{i}") for i in range(2)]
            s_v = [sem(f"v_loaded{i}") for i in range(2)]
            s_res = [sem(f"residual_loaded{i}") for i in range(2)]
            s_bm = [sem(f"bias_rows_loaded{i}") for i in range(4)]
            s_md = [sem(f"max_rows_placed{i}") for i in range(2)]
            s_x1 = [sem(f"x1_stored{i}") for i in range(2)]
            s_xns = [sem(f"xn2_stored{i}") for i in range(2)]
            s_list = [sem(f"entries_stored{i}") for i in range(2)]
            s_qk = sem("logits_ready")
            s_exp = sem("probs_ready")
            s_pv = sem("pv_done")
            s_out = sem("attention_copied")
            s_rsum = sem("sums_inverted")
            s_x1a = sem("x1_columns")
            s_m = sem("max_logits_ready")
            s_mx = sem("maxima_taken")
            s_nm = sem("neg_max_split")
            s_stat = sem("ln1_stats")
            s_xg = sem("q_normalised")
            s_hi = sem("hi_parts")
            s_lo = sem("lo_parts")
            s_ln2 = sem("ln2_steps")
            s_route = sem("route_steps")
            s_gexp = sem("gate_exp")
            s_msum = sem("counts_added")
            s_disp = sem("dispatch_steps")
            s_turn = [sem(f"turned{i}") for i in range(2)]
            s_took = [sem(f"turn_taken{i}") for i in range(2)]

            def turn_of(st, name, off=0):
                if st.rnd is None:
                    k = turns[(st.l + off, name)]
                    return k % 2, k // 2
                k = turns[(STEPS_IN_BODY + st.l + off, name)]
                return k % 2, st.rnd * (per_round // 2) + (k // 2 - per_round // 2)

            def put_turn(eng, st, name):
                i, before = turn_of(st, name)
                eng.wait_ge(s_took[i], before)
                return psT[i], s_turn[i]

            def take_turn(eng, st, name):
                i, before = turn_of(st, name)
                eng.wait_ge(s_turn[i], before + 1)
                return psT[i], s_took[i]

            def all_steps(eng, step):
                for n in range(FIRST, 8):
                    step(Step(None, n, G))
                with eng.Fori(1, G // STEPS_IN_BODY - 1) as rnd:
                    for l in range(STEPS_IN_BODY):
                        step(Step(rnd, l, G))
                for n in range(G - STEPS_IN_BODY, G + LAST):
                    step(Step(None, n, G))

            block = ctx.enter_context(nc.Block())

            @block.sync
            def _(sp):
                def step(st):
                    if st.g() == 0:
                        par = (st.l // 4) % 2
                        if st.on(8):
                            if st.rnd is not None or st.l >= 0:
                                sp.wait_ge(s_lo, st.count(2, 4, 0))
                            b = st.batch(1, 8, 0)
                            sp.dma_start(xin[:, par, :, :], x_d[bass.ds(b, 1)].rearrange("a p i d -> p (a i) d")).then_inc(s_x[par], 16)
                            sp.dma_start(kin[:, par, :, :], c_d[bass.ds(b, 1), :, :, 0:D].rearrange("a p i d -> p (a i) d")).then_inc(s_k[par], 16)
                        if st.on(0):
                            if st.rnd is not None or st.l >= 8:
                                sp.wait_ge(s_x1[par], st.bpair(16, 0, 0))
                                sp.wait_ge(s_ln2, st.count(LN2, -4, 0))
                            b = st.batch(1, 0, 0)
                            sp.dma_start(xres[:, par, :, :], x_d[bass.ds(b, 1)].rearrange("a p i d -> p (a i) d")).then_inc(s_res[par], 16)
                    if st.g() == 1 and st.on(4):
                        par = (st.l // 4 + 1) % 2
                        if st.rnd is not None or st.l >= 4:
                            sp.wait_ge(s_pv, st.batch(16, 0, 0))
                        b = st.batch(1, 4, 0)
                        sp.dma_start(vin[:, par, :, :], c_d[bass.ds(b, 1), :, :, D:2 * D].rearrange("a p i d -> p (a i) d")).then_inc(s_v[par], 16)
                    if st.on(3):
                        g = st.g(3)
                        if st.rnd is not None or st.l >= 1:
                            sp.wait_ge(s_qk, st.count(16, 0, 0))
                        b = st.batch(1, 3, 0)
                        for j in range(HG):
                            sp.dma_start(stA[96:98, g, j, :].bitcast(F32), bm_d[bass.ds(b, 1)].rearrange("a t s -> (a t) s")).then_inc(s_bm[g], 16)
                    if st.on(1):
                        i, before = turn_of(st, "MT")
                        sp.wait_ge(s_took[i], before + 1)
                        for t in range(2):
                            sp.dma_start(stB[98 + t:99 + t, st.g(1), :, :].bitcast(F32), mT[HG * t:HG * t + HG, :].bitcast(F32)).then_inc(s_md[(st.l + 1) % 2], 16)
                    if st.g() == 1 and st.on(-5):
                        par = (st.l // 4 + 1) % 2
                        sp.wait_ge(s_x1a, st.batch(4, -4, 4))
                        b = st.batch(1, -4, 0)
                        sp.dma_start(out_d[bass.ds(b, 1)].rearrange("a p i d -> p (a i) d"), xres[:, par, :, :]).then_inc(s_x1[par], 16)
                    if st.on(-4):
                        sp.wait_ge(s_ln2, st.count(LN2, -4, LN2))
                        t = st.count(1, -4, 0)
                        sp.dma_start(xn_d.rearrange("(t p) d -> t p d", p=P)[bass.ds(t, 1)].rearrange("a p d -> (a p) d"),
                                     xn2[:, st.l % 2, :]).then_inc(s_xns[st.l % 2], 16)

                all_steps(sp, step)
                for i in range(2):
                    sp.wait_ge(s_x1[i], 16 * (B // 2))
                    sp.wait_ge(s_xns[i], 16 * (G // 2))

            @block.gpsimd
            def _(pool):
                def step(st):
                    if st.on(4):
                        r = st.l % 2
                        q3 = rowQ[:, r, :, :, :].rearrange("p i h c -> p (i h) c")
                        k3 = rowK[:, r, :, :, :].rearrange("p i h c -> p (i h) c")
                        pool.wait_ge(s_xg, st.count(4, 4, 4))
                        pool.wait_ge(s_hi, st.count(2, 4, 1))
                        pool.tensor_tensor(q3[:, :, 2 * DH:W3], xg[:, r, :, :].rearrange("p i (h c) -> p (i h) c", c=DH),
                                           q3[:, :, 0:DH].bitcast(F32), ALU.subtract).then_inc(s_lo, 1)
                        kpar = ((st.l + 4) // 4) % 2
                        ksrc = kin[:, kpar, :, st.g() * P:(st.g() + 1) * P]
                        pool.wait_ge(s_hi, st.count(2, 4, 2))
                        pool.tensor_tensor(rowK[:, r, :, :, DH:2 * DH], ksrc.rearrange("p i (h c) -> p i h c", c=DH),
                                           rowK[:, r, :, :, 0:DH].bitcast(F32), ALU.subtract).then_inc(s_lo, 1)
                    if st.on(-6):
                        r = st.l % 2
                        pool.wait_ge(s_disp, st.count(7, -6, 7))
                        if st.rnd is not None:
                            pool.tensor_tensor(hold[:, 3 + r:4 + r], ones[:, 0:1], ones[:, 0:1], ALU.add)
                        for e in range(E):
                            pool.indirect_dma_start(list_d, bass.IndirectOffsetOnAxis(ap=slot[:, r, e:e + 1], axis=0),
                                                    entry[:, r, e, :], None, bounds_check=LIST - 1,
                                                    oob_is_err=False).then_inc(s_list[r], 16)

                all_steps(pool, step)
                for i in range(2):
                    pool.wait_ge(s_list[i], 16 * E * (G // 2))

            @block.scalar
            def _(act):
                def evac_stack(st, k):
                    side, j, g = k % 2, k // 2, st.g(3)
                    if k == 0:
                        if st.rnd is not None or st.l >= 1:
                            act.wait_ge(s_qk, st.count(16, 0, 0))
                    bank, took = take_turn(act, st, f"T{k}")
                    dst = (stB, stA)[side]
                    act.activation(dst[0:W3, g, j, :], bank[0:W3, :], ACT.Copy).then_inc(took, 1)

                def step(st):
                    for s in range(16):
                        u, j = s // 4, s % 4
                        if st.on(0):
                            if j == 0 and (u >= 2 or st.rnd is not None or st.l >= 1):
                                act.wait_ge(s_pv, st.count(4, 0, u - 1))
                            act.wait_ge(s_qk, st.count(16, 0, s + 1))
                            act.activation(prob[:, u % 2, j, :], psS[j % 2][:, :], ACT.Exp).then_inc(s_exp, 1)
                        if j % 2 == 0 and st.on(3):
                            evac_stack(st, 2 * u + j // 2)
                        if s == 1 and st.on(-5):
                            bank, took = take_turn(act, st, "XT")
                            act.activation(xT[:, :, :].rearrange("p k t -> p (k t)"), bank[:, :], ACT.Copy).then_inc(took, 1)
                        if s == 3 and st.on(1):
                            if st.rnd is not None or st.l >= 0:
                                act.wait_ge(s_md[st.l % 2], st.pair(32, 0, 32))
                            bank, took = take_turn(act, st, "MT")
                            act.activation(mT[:, :], bank[0:2 * HG, :], ACT.Copy).then_inc(took, 1)
                        if s in (2, 3) and st.on(-1):
                            if s == 2:
                                act.wait_ge(s_pv, st.count(4, -1, 4))
                            if st.rnd is not None or st.l - 1 >= 2:
                                b, before = turn_of(st, "DT" if s == 2 else "OT", -2)
                                act.wait_ge(s_turn[b], before + 1)
                            dst, src = ((sumT, psD), (attT, psO))[s - 2]
                            act.activation(dst[:, (st.l + 1) % 2, :], src[:, :], ACT.Copy).then_inc(s_out, 1)
                        if s == 15 and st.on(-5):
                            act.wait_ge(s_route, st.count(5, -5, 5))
                            act.activation(expo[:, (st.l + 1) % 2, :], shifted[:, (st.l + 1) % 2, :], ACT.Exp).then_inc(s_gexp, 1)

                all_steps(act, step)

            @block.tensor
            def _(pe):
                def pv(st, off, u):
                    kt = NT - 1 - u
                    g = st.g(off)
                    vpar = ((st.l + off) // 4) % 2
                    pe.wait_ge(s_exp, st.count(16, off, 4 * u + 4))
                    if u == 0:
                        pe.wait_ge(s_v[vpar], st.bpair(16, off, 16))
                        if st.rnd is not None or st.l + off >= 1:
                            pe.wait_ge(s_out, st.count(2, off, 0))
                    for bank, w in ((psO, None), (psD, ones)):
                        for j in range(HG):
                            c0 = (HG * g + j) * DH
                            lhs = vin[:, vpar, kt, c0:c0 + DH] if w is None else w[:, 0:DH]
                            last = pe.matmul(bank[DH * j:DH * (j + 1), :], lhs, prob[:, u % 2, j, :],
                                             start=(u == 0), stop=(u == NT - 1), skip_group_check=True,
                                             tile_position=(0, DH * j))
                    last.then_inc(s_pv, 1)

                def turn_rows(st, k):
                    side, j = k % 2, k // 2
                    r = (st.l + 3) % 2
                    if k == 0:
                        pe.wait_ge(s_hi, st.count(2, 3, 2))
                        pe.wait_ge(s_lo, st.count(2, 3, 2))
                    bank, done = put_turn(pe, st, f"T{k}")
                    src = (rowQ, rowK)[side]
                    for i in range(NT):
                        last = pe.transpose(bank[0:W3, i * P:(i + 1) * P], src[:, r, i, j, :].bitcast(F32), ident[:, :])
                    last.then_inc(done, 1)

                def step(st):
                    for s in range(16):
                        u, j = s // 4, s % 4
                        if st.on(0):
                            kt, g = NT - 1 - u, st.g()
                            if s == 0:
                                pe.wait_ge(s_md[st.l % 2], st.pair(32, 0, 32))
                            if s >= 2 or st.rnd is not None or st.l >= 1:
                                pe.wait_ge(s_exp, st.count(16, 0, s - 1))
                            pe.matmul(psS[j % 2][:, :], stA[0:100, g, j, kt * P:(kt + 1) * P], stB[0:100, g, j, :],
                                      start=True, stop=True).then_inc(s_qk, 1)
                        if st.on(2):
                            i, g = s // 4, st.g(2)
                            if s == 0:
                                pe.wait_ge(s_bm[g], st.batch(64, 2, 64))
                                for name in ("T6", "T7"):
                                    b, before = turn_of(st, name, -1)
                                    pe.wait_ge(s_took[b], before + 1)
                            if s >= 2 or st.rnd is not None or st.l + 2 >= 1:
                                pe.wait_ge(s_mx, st.count(16, 2, s - 1))
                            pe.matmul(psM[s % 2][:, :], stB[0:98, g, j, i * P:(i + 1) * P], stA[0:98, g, j, :],
                                      start=True, stop=True).then_inc(s_m, 1)
                        if j == 1:
                            if u > 0 and st.on(0):
                                pv(st, 0, u - 1)
                            if u == 0 and st.on(-1):
                                pv(st, -1, NT - 1)
                        if j % 2 == 0 and st.on(3):
                            turn_rows(st, 2 * u + j // 2)
                        if s == 1 and st.on(-5):
                            pe.wait_ge(s_ln2, st.count(LN2, -5, LN2))
                            bank, done = put_turn(pe, st, "XT")
                            for k in range(KD):
                                last = pe.transpose(bank[:, k * P:(k + 1) * P], xn2[:, (st.l + 1) % 2, k * P:(k + 1) * P], ident[:, :])
                            last.then_inc(done, 1)
                        if s == 3 and st.on(1):
                            pe.wait_ge(s_nm, st.count(2, 1, 2))
                            bank, done = put_turn(pe, st, "MT")
                            for i in range(NT):
                                last = pe.transpose(bank[0:2 * HG, i * P:(i + 1) * P],
                                                    nm[:, i, :, :].rearrange("p t h -> p (t h)").bitcast(F32), ident[:, :])
                            last.then_inc(done, 1)
                        if s == 5 and st.on(-6):
                            pe.wait_ge(s_route, st.count(5, -6, 5))
                            if st.rnd is not None or st.l >= 7:
                                pe.wait_ge(s_msum, st.count(1, -6, 0))
                            bank, done = put_turn(pe, st, "RK")
                            pe.matmul(bank[:, 0:E], lower[:, :], mask[:, st.l % 2, :], start=True, stop=False)
                            pe.matmul(bank[:, 0:E], ones[:, :], msum[:, :], start=False, stop=True).then_inc(done, 1)
                        if s in (5, 7) and st.on(-1):
                            name, src = ("DT", sumT) if s == 5 else ("OT", attT)
                            pe.wait_ge(s_out, st.count(2, -1, 1 if s == 5 else 2))
                            bank, done = put_turn(pe, st, name)
                            for i in range(NT):
                                last = pe.transpose(bank[:, i * P:(i + 1) * P], src[:, (st.l + 1) % 2, i * P:(i + 1) * P], ident[:, :])
                            last.then_inc(done, 1)
                        if s == 9 and st.on(-5):
                            b, before = turn_of(st, "XT")
                            pe.wait_ge(s_took[b], before + 1)
                            bank, done = put_turn(pe, st, "LG")
                            for k in range(KD):
                                last = pe.matmul(bank[:, 0:2 * E], xT[:, k, :], routeT[:, k, :], start=(k == 0), stop=(k == KD - 1))
                            last.then_inc(done, 1)

                all_steps(pe, step)

            @block.vector
            def _(dve):
                def ln2(st, s):
                    i, par = st.g(), ((st.l + 4) // 4) % 2
                    src = xres[:, par, i, :]
                    c = lambda k: st.count(LN2, -4, k)
                    if s == 10:
                        dve.wait_ge(s_x1a, st.batch(4, -4, 4))
                        dve.bn_stats(st6b[:, :], src).then_inc(s_ln2, 1)
                    if s == 11:
                        dve.wait_ge(s_ln2, c(1))
                        dve.memset(hold[:, 0:1], 0.0)
                        dve.bn_aggr(mvb[:, :], st6b[:, :]).then_inc(s_ln2, 1)
                        dve.wait_ge(s_ln2, c(2))
                        dve.tensor_scalar(varb[:, 0:1], mvb[:, 1:2], LN_EPS, None, ALU.add).then_inc(s_ln2, 1)
                        dve.tensor_copy(varb[:, 1:2], mvb[:, 1:2]).then_inc(s_ln2, 1)
                    if s == 12:
                        dve.wait_ge(s_ln2, c(4))
                    if 12 <= s <= 15:
                        rsqrt(dve, rsb[:, :], rst[:, :], varb[:, :], s_ln2, lambda k: c(4 + k),
                              (0, 4, 7, 10)[s - 12], (4, 7, 10, RSQRT_STEPS)[s - 12])
                    if s == 16:
                        if st.rnd is not None or st.l - 4 >= 2:
                            dve.wait_ge(s_xns[st.l % 2], st.pair(16, -4, 0))
                        dve.wait_ge(s_ln2, c(4 + RSQRT_STEPS))
                        dve.tensor_scalar(nrm[:, 1:2], mvb[:, 1:2], rsb[:, 1:2], float(D) ** 0.5, ALU.mult, ALU.mult).then_inc(s_ln2, 1)
                        dve.tensor_scalar(xn2[:, st.l % 2, :], src, mvb[:, 0:1], rsb[:, 0:1], ALU.subtract, ALU.mult).then_inc(s_ln2, 1)
                        dve.wait_ge(s_ln2, c(LN2 - 2))
                        dve.tensor_scalar(nrm[:, 0:1], nrm[:, 1:2], rsb[:, 0:1], NORM_EPS, ALU.mult, ALU.max).then_inc(s_ln2, 1)

                def route(st, s):
                    r = (st.l + 1) % 2
                    c = lambda k: st.count(5, -5, k)
                    if s == 10:
                        dve.wait_ge(s_ln2, st.count(LN2, -5, LN2))
                        dve.reciprocal(gsum[:, 1:2], nrm[:, 0:1]).then_inc(s_route, 1)
                        bank, took = take_turn(dve, st, "LG")
                        dve.tensor_copy(lg[:, :], bank[:, 0:2 * E]).then_inc(took, 1)
                    if s == 11:
                        dve.wait_ge(s_route, c(1))
                        b, before = turn_of(st, "LG")
                        dve.wait_ge(s_took[b], before + 1)
                        dve.scalar_tensor_tensor(out=logit[:, :], in0=lg[:, 0:E], scalar=gsum[:, 1:2], in1=lg[:, E:2 * E],
                                                 op0=ALU.mult, op1=ALU.add).then_inc(s_route, 1)
                    if s == 12:
                        dve.wait_ge(s_route, c(2))
                        dve.memset(hold[:, 1:2], 0.0)
                        dve.max(top8[:, :], logit[:, :]).then_inc(s_route, 1)
                    if s == 13:
                        dve.wait_ge(s_route, c(3))
                        dve.tensor_scalar(mask[:, r, :], logit[:, :], top8[:, 1:2], None, ALU.is_ge).then_inc(s_route, 1)
                        dve.tensor_scalar(shifted[:, r, :], logit[:, :], top8[:, 0:1], None, ALU.subtract).then_inc(s_route, 1)

                def dispatch(st, s):
                    r = st.l % 2
                    c = lambda k: st.count(7, -6, k)
                    if s == 5:
                        if st.rnd is not None or st.l - 6 >= 2:
                            dve.wait_ge(s_list[r], st.pair(16 * E, -6, 0))
                        if st.rnd is not None or st.l - 6 >= 1:
                            dve.wait_ge(s_disp, c(0))
                        dve.wait_ge(s_gexp, st.count(1, -6, 1))
                        dve.tensor_tensor_reduce(chosen[:, :], expo[:, r, :], mask[:, r, :], 1.0, 0.0, ALU.mult, ALU.add,
                                                 gsum[:, 0:1]).then_inc(s_disp, 1)
                    if s == 6:
                        bank, took = take_turn(dve, st, "RK")
                        dve.tensor_tensor(slot_f[:, :], bank[:, 0:E], e_off[:, :], ALU.add).then_inc(took, 1)
                        dve.wait_ge(s_disp, c(1))
                        dve.reciprocal(gsum[:, 0:1], gsum[:, 0:1]).then_inc(s_disp, 1)
                        dve.tensor_tensor(msum[:, :], msum[:, :], mask[:, r, :], ALU.add).then_inc(s_msum, 1)
                    if s == 7:
                        b, before = turn_of(st, "RK")
                        dve.wait_ge(s_took[b], before + 1)
                        dve.tensor_tensor(slot_f[:, :], slot_f[:, :], mask[:, r, :], ALU.mult).then_inc(s_disp, 1)
                        dve.wait_ge(s_disp, c(2))
                        dve.tensor_scalar(entry[:, r, :, 1].bitcast(F32), chosen[:, :], gsum[:, 0:1], tanh_f[:, 0:1],
                                          ALU.mult, ALU.mult).then_inc(s_disp, 1)
                    if s == 8:
                        dve.wait_ge(s_disp, c(3))
                        dve.tensor_scalar(slot[:, r, :], slot_f[:, :], FAR, None, ALU.add).then_inc(s_disp, 1)
                        dve.tensor_scalar(entry[:, r, :, 0], mask[:, r, :], 0.0, token[:, 0:1], ALU.mult, ALU.add).then_inc(s_disp, 1)
                        dve.wait_ge(s_disp, c(6))
                        dve.tensor_scalar(token[:, :], token[:, :], float(P), None, ALU.add).then_inc(s_disp, 1)

                def stats(st, i):
                    par = (st.l // 4) % 2
                    if i == 0:
                        dve.wait_ge(s_x[par], st.bpair(16, 8, 16))
                    dve.bn_stats(st6[:, i, :], xin[:, par, i, :]).then_inc(s_stat, 1)
                    dve.wait_ge(s_stat, st.batch(LN1, 8, 2 * i + 1))
                    dve.memset(hold[:, 2:3], 0.0)
                    dve.bn_aggr(mv[:, i, :], st6[:, i, :]).then_inc(s_stat, 1)

                def scale(st, s):
                    par = (st.l // 4) % 2
                    c = lambda k: st.batch(LN1, 8, k)
                    if s == 0:
                        dve.wait_ge(s_stat, c(8))
                        dve.tensor_copy(mean[:, par, :], mv[:, :, 0])
                        dve.tensor_scalar(varx[:, :], mv[:, :, 1], LN_EPS, None, ALU.add).then_inc(s_stat, 1)
                    if s == 1:
                        dve.wait_ge(s_stat, c(9))
                    if 1 <= s <= RSQRT_STEPS:
                        rsqrt(dve, rstd[:, par, :], varx2[:, :], varx[:, :], s_stat, lambda k: c(9 + k), s - 1, s)
                    if s == 14:
                        dve.wait_ge(s_stat, c(9 + RSQRT_STEPS))
                        dve.tensor_scalar(rstd[:, par, :], rstd[:, par, :], live[:, bass.ds(st.batch(1, 8, 0), 1)],
                                          float(DH) ** -0.5, ALU.mult, ALU.mult).then_inc(s_stat, 1)

                def rows(st, part):
                    r, g, par = st.l % 2, st.g(), ((st.l + 4) // 4) % 2
                    if part == 0:
                        dve.wait_ge(s_stat, st.batch(LN1, 4, LN1))
                        if st.rnd is not None or st.l + 4 >= 2:
                            dve.wait_ge(s_lo, st.count(2, 3, 0))
                    if part in (0, 1):
                        for i in range(2 * part, 2 * part + 2):
                            dve.tensor_scalar(xg[:, r, i, :], xin[:, par, i, g * P:(g + 1) * P], mean[:, par, i:i + 1],
                                              rstd[:, par, i:i + 1], ALU.subtract, ALU.mult).then_inc(s_xg, 1)
                    if part == 2:
                        if st.rnd is not None or st.l + 4 >= 2:
                            for name in ("T6", "T7"):
                                b, before = turn_of(st, name, -1)
                                dve.wait_ge(s_turn[b], before + 1)
                        dve.wait_ge(s_xg, st.count(4, 4, 4))
                        dst = rowQ[:, r, :, :, 0:2 * DH].rearrange("p i h (t c) -> p (i h) t c", t=2)
                        src = xg[:, r, :, :].rearrange("p i (h a c) -> p (i h) a c", a=1, c=DH).to_broadcast([P, NT * HG, 2, DH])
                        dve.tensor_copy(dst, src).then_inc(s_hi, 1)
                    if part in (3, 4):
                        t = 2 * (part - 3)
                        if part == 3:
                            dve.wait_ge(s_k[par], st.bpair(16, 4, 16))
                        ins = dve.tensor_copy(rowK[:, r, :, :, t * DH:(t + 1) * DH],
                                              kin[:, par, :, g * P:(g + 1) * P].rearrange("p i (h c) -> p i h c", c=DH))
                        if part == 4:
                            ins.then_inc(s_hi, 1)

                def step(st):
                    for s in range(16):
                        if st.on(2):
                            if s == 0 and (st.rnd is not None or st.l + 2 >= 1):
                                dve.wait_ge(s_nm, st.count(2, 2, 0))
                            dve.wait_ge(s_m, st.count(16, 2, s + 1))
                            dve.tensor_reduce(mx[:, s // 4, s % 4:s % 4 + 1], psM[s % 2][:, :], AX.X, ALU.max).then_inc(s_mx, 1)
                        if s <= 4 and st.on(4):
                            rows(st, s)
                        if s == 6 and st.on(-1):
                            bank, took = take_turn(dve, st, "DT")
                            sums = bank[:, :].rearrange("p (i h c) -> p i h c", i=NT, h=HG)[:, :, :, 0]
                            dve.reciprocal(rsum[:, :, :], sums).then_inc(took, 1)
                        if s == 7 and st.on(-1):
                            b, before = turn_of(st, "DT")
                            dve.wait_ge(s_took[b], before + 1)
                            dve.tensor_scalar(rsum[:, :, :], rsum[:, :, :], tanh_a[:, 0:1], None, ALU.mult).then_inc(s_rsum, 1)
                        if 5 <= s <= 8 and st.on(-6):
                            dispatch(st, s)
                        if s == 8 and st.on(-1):
                            dve.wait_ge(s_rsum, st.count(1, -1, 1))
                            bank, took = take_turn(dve, st, "OT")
                            each = rsum[:, :, :].rearrange("p i (h a) -> p (i h) a", a=1).to_broadcast([P, NT * HG, DH])
                            dve.tensor_tensor(scaled[:, :, :].rearrange("p i (h c) -> p (i h) c", h=HG),
                                              bank[:, :].rearrange("p (h c) -> p h c", c=DH), each, ALU.mult).then_inc(took, 1)
                        if s == 9 and st.on(-1):
                            g, par = st.g(-1), ((st.l - 1) // 4) % 2
                            if g == 0:
                                dve.wait_ge(s_res[par], st.bpair(16, -1, 16))
                            b, before = turn_of(st, "OT")
                            dve.wait_ge(s_took[b], before + 1)
                            dst = xres[:, par, :, g * P:(g + 1) * P]
                            dve.tensor_tensor(dst, dst, scaled[:, :, :], ALU.add).then_inc(s_x1a, 1)
                        if 10 <= s <= 13 and st.on(-5):
                            route(st, s)
                        if 10 <= s and st.on(-4):
                            ln2(st, s)
                        if st.g() in (1, 2) and s in (13, 14) and st.on(8 - st.g()):
                            stats(st, 2 * (st.g() - 1) + s - 13)
                        if st.g() == 3 and s <= 14 and st.on(5):
                            scale(st, s)
                    if st.on(-4):
                        ln2(st, 16)
                    if st.on(2):
                        dve.wait_ge(s_mx, st.count(16, 2, 16))
                        if st.rnd is not None or st.l + 2 >= 1:
                            b, before = turn_of(st, "MT")
                            dve.wait_ge(s_turn[b], before + 1)
                        dve.tensor_scalar(nm[:, :, 0, :], mx[:, :, :], -1.0, None, ALU.mult).then_inc(s_nm, 1)
                        dve.wait_ge(s_nm, st.count(2, 2, 1))
                        dve.scalar_tensor_tensor(out=nm[:, :, 1, :], in0=mx[:, :, :], scalar=-1.0,
                                                 in1=nm[:, :, 0, :].bitcast(F32), op0=ALU.mult, op1=ALU.subtract).then_inc(s_nm, 1)

                all_steps(dve, step)

        with ExitStack() as ctx:
            def sb(name, shape, dt=F32):
                return ctx.enter_context(nc.sbuf_tensor(name, shape, dt))

            def ps(name, shape):
                return ctx.enter_context(nc.psum_tensor(name, shape, F32))

            NS = BLK // P
            w1s = sb("w1s", [P, 2, KD, DE])
            w2s = sb("w2s", [P, 2, KE, D])
            b1s = sb("b1s", [P, 2, KE])
            b2s = sb("b2s", [P, 2, D])
            ids = sb("ids", [P, 2, NS, 2], I32)
            rows = sb("rows_in", [P, 2, NS, D])
            xTb = sb("xTb", [P, 2, KD, BLK])
            hT = sb("hT", [P, 2, KE, BLK])
            ysum = sb("ysum", [P, 2, D])
            yout = sb("yout", [P, 2, NS, D])
            cnt = sb("cnt", [P, E])
            nblk = sb("nblk", [P, E])
            cum = sb("cum", [P, 2, E])
            qcol_i = sb("qcol_i", [P, 1], I32)
            qcol = sb("qcol", [P, 1])
            before = sb("before", [P, E])
            scr8 = sb("scr8", [P, E])
            place = sb("place", [P, 6])
            tab_i = sb("tab_i", [P, 2], I32)
            banks = [ps(f"bankb{i}", [P, 512]) for i in range(8)]
            psT, psH, psY = banks[0:2], banks[2:4], banks[4:8]

            t_pe = sem("table_counts")
            t_dve = sem("table_steps")
            t_pool = sem("table_iota")
            t_sp = sem("table_moved")
            with nc.Block() as block:
                @block.tensor
                def _(pe):
                    pe.matmul(psT[0][:, 0:E], ones[:, :], msum[:, :], start=True, stop=True).then_inc(t_pe, 1)

                @block.gpsimd
                def _(pool):
                    pool.iota(qcol_i[:, :], pattern=[[0, 1]], base=0, channel_multiplier=1).then_inc(t_pool, 1)

                @block.vector
                def _(dve):
                    done = 0

                    def then(ins):
                        nonlocal done
                        done += 1
                        ins.then_inc(t_dve, 1)
                        dve.wait_ge(t_dve, done)

                    dve.memset(rows[:, :, :, :], 0.0)
                    for t in range(2):
                        dve.memset(tab[0:1, 2 * (P + t):2 * (P + t) + 1], LIST)
                        dve.memset(tab[0:1, 2 * (P + t) + 1:2 * (P + t) + 2], E - 1)
                    dve.wait_ge(t_pe, 1)
                    dve.wait_ge(t_pool, 1)
                    then(dve.tensor_copy(qcol[:, :], qcol_i[:, :]))
                    then(dve.tensor_scalar(cnt[:, :], psT[0][:, 0:E], (BLK - 1) / 2.0, 1.0 / BLK, ALU.add, ALU.mult))
                    then(dve.tensor_scalar(cnt[:, :], cnt[:, :], ROUND, None, ALU.add))
                    then(dve.tensor_scalar(nblk[:, :], cnt[:, :], ROUND, None, ALU.subtract))
                    then(dve.tensor_copy(cum[:, 0, :], nblk[:, :]))
                    src = 0
                    for k in (1, 2, 4):
                        then(dve.tensor_copy(cum[:, 1 - src, 0:k], cum[:, src, 0:k]))
                        then(dve.tensor_tensor(cum[:, 1 - src, k:E], cum[:, src, k:E], cum[:, src, 0:E - k], ALU.add))
                        src = 1 - src
                    then(dve.tensor_scalar(before[:, :], cum[:, src, :], qcol[:, 0:1], None, ALU.is_le))
                    then(dve.tensor_reduce(place[:, 0:1], before[:, :], AX.X, ALU.add))
                    then(dve.tensor_tensor_reduce(scr8[:, :], before[:, :], nblk[:, :], 1.0, 0.0, ALU.mult, ALU.add,
                                                  place[:, 1:2]))
                    then(dve.tensor_tensor(place[:, 2:3], qcol[:, :], place[:, 1:2], ALU.subtract))
                    then(dve.tensor_scalar(place[:, 2:3], place[:, 2:3], float(BLK), None, ALU.mult))
                    then(dve.tensor_scalar(place[:, 3:4], place[:, 0:1], float(CAP), place[:, 2:3], ALU.mult, ALU.add))
                    then(dve.tensor_scalar(tab_i[:, 0:1], place[:, 3:4], float(LIST), None, ALU.min))
                    then(dve.tensor_scalar(tab_i[:, 1:2], place[:, 0:1], float(E - 1), None, ALU.min))
                    then(dve.tensor_scalar(place[:, 4:5], cum[:, src, E - 1:E], 0.5, 0.25, ALU.mult, ALU.add))
                    then(dve.tensor_scalar(place[:, 5:6], place[:, 4:5], ROUND, None, ALU.add))
                    then(dve.tensor_scalar(tab[0:1, N_ROUNDS:N_ROUNDS + 1], place[0:1, 5:6], ROUND, None, ALU.subtract))

                @block.sync
                def _(sp):
                    sp.wait_ge(t_dve, 19)
                    sp.dma_start(tab_d, tab_i[:, :]).then_inc(t_sp, 16)
                    sp.wait_ge(t_sp, 16)
                    sp.dma_start(tab[0:1, 0:2 * P], tab_d.rearrange("(a q) t -> a (q t)", a=1)).then_inc(t_sp, 16)
                    sp.wait_ge(t_sp, 32)

            f_ids = [sem(f"ids_loaded{i}") for i in range(2)]
            f_w = [sem(f"weights_loaded{i}") for i in range(2)]
            f_rows = [sem(f"rows_gathered{i}") for i in range(2)]
            f_add = [sem(f"rows_added{i}") for i in range(2)]
            f_hold = sem("pool_held")
            f_xt = sem("rows_turned")
            f_xs = sem("turned_taken")
            f_h = sem("hidden_ready")
            f_g = sem("gelu_done")
            f_y = sem("out_ready")
            f_s = sem("bias_added")
            f_o = sem("gate_applied")

            adds = [(f_hold, 6), (f_xt, 2 * KD), (f_xs, 2 * KD), (f_h, 2 * KE), (f_g, 2 * KE), (f_y, 2 * NS),
                    (f_s, 2 * NS), (f_o, 2 * NS)]
            with nc.Block() as block:
                @block.sync
                def _(sp):
                    for start_of, count in adds:
                        sp.sem_inc(start_of, count)

            def n_rounds(eng):
                return eng.value_load(tab[0:1, N_ROUNDS:N_ROUNDS + 1], min_val=1, max_val=P // 2)

            def rounds(eng):
                return eng.Fori(1, n_rounds(eng) + 1)

            with nc.Block() as block:
                @block.sync
                def _(sp):
                    def load(h, at):
                        start = sp.value_load(tab[0:1, bass.ds(at, 1)], min_val=0, max_val=LIST)
                        expert = sp.value_load(tab[0:1, bass.ds(at + 1, 1)], min_val=0, max_val=E - 1)
                        sp.dma_start(ids[:, h, :, :], list_d[bass.ds(start, BLK), :].rearrange("(c p) t -> p c t", p=P)).then_inc(f_ids[h], 16)
                        sp.dma_start(w1s[:, h, :, :], w1[bass.ds(expert, 1)].rearrange("a (k p) n -> p (a k) n", p=P)).then_inc(f_w[h], 16)
                        sp.dma_start(b1s[:, h, :], b1[bass.ds(expert, 1)].rearrange("a (k p) -> p (a k)", p=P),
                                     allow_slow_non_contiguous=True).then_inc(f_w[h], 16)
                        sp.dma_start(w2s[:, h, :, :], w2[bass.ds(expert, 1)].rearrange("a (k p) n -> p (a k) n", p=P)).then_inc(f_w[h], 16)
                        sp.dma_start(b2s[:, h, :], b2[bass.ds(expert, 1), :].to_broadcast([P, D])).then_inc(f_w[h], 16)

                    load(0, 0)
                    load(1, 2)
                    with rounds(sp) as r:
                        for h in range(2):
                            sp.wait_ge(f_hold, r * 6 + (3 * h + 3))
                            load(h, r * 4 + 2 * h)

                @block.gpsimd
                def _(pool):
                    def carry_wait():
                        pool.tensor_tensor(hold[:, 5:6], ones[:, 0:1], ones[:, 0:1], ALU.add).then_inc(f_hold, 1)

                    def gather(h):
                        for c in range(NS):
                            pool.indirect_dma_start(rows[:, h, c, :], None, xn_d,
                                                    bass.IndirectOffsetOnAxis(ap=ids[:, h, c, 0:1], axis=0),
                                                    bounds_check=TOK - 1, oob_is_err=False).then_inc(f_rows[h], 16)

                    pool.wait_ge(f_ids[0], 16)
                    gather(0)
                    with rounds(pool) as r:
                        for h in range(2):
                            pool.wait_ge(f_hold, r * 6 + 3 * h)
                            pool.wait_ge(f_ids[1 - h], r * 16 + 16 * h)
                            pool.wait_ge(f_xt, r * (2 * KD) + KD * h)
                            carry_wait()
                            gather(1 - h)
                            pool.wait_ge(f_hold, r * 6 + (3 * h + 1))
                            pool.wait_ge(f_o, r * (2 * NS) + (NS * h + NS))
                            carry_wait()
                            for c in range(NS):
                                pool.indirect_dma_start(out_rows, bass.IndirectOffsetOnAxis(ap=ids[:, h, c, 0:1], axis=0),
                                                        yout[:, h, c, :], None, bounds_check=TOK - 1, oob_is_err=False,
                                                        compute_op=ALU.add).then_inc(f_add[h], 16)
                            pool.wait_ge(f_hold, r * 6 + (3 * h + 2))
                            pool.wait_ge(f_add[h], r * (16 * NS))
                            carry_wait()
                    n = n_rounds(pool)
                    for h in range(2):
                        pool.wait_ge(f_ids[h], n * 16 + 16)
                        pool.wait_ge(f_w[h], n * 64 + 64)
                    pool.wait_ge(f_rows[0], n * (16 * NS) + 16 * NS)

                @block.tensor
                def _(pe):
                    with rounds(pe) as r:
                        for h in range(2):
                            pe.wait_ge(f_rows[h], r * (16 * NS))
                            for k in range(KD):
                                pe.wait_ge(f_xs, r * 8 + (4 * h + k - 1) if 4 * h + k >= 1 else r * 8)
                                for c in range(NS):
                                    last = pe.transpose(psT[k % 2][:, c * P:(c + 1) * P], rows[:, h, c, k * P:(k + 1) * P], ident[:, :])
                                last.then_inc(f_xt, 1)
                            pe.wait_ge(f_w[h], r * 64)
                            for m in range(KE):
                                if m == 0:
                                    pe.wait_ge(f_g, r * 4 + 2 * h)
                                for k in range(KD):
                                    if m == 0:
                                        pe.wait_ge(f_xs, r * 8 + (4 * h + k + 1))
                                    last = pe.matmul(psH[m][:, :], w1s[:, h, k, m * P:(m + 1) * P], xTb[:, h, k, :],
                                                     start=(k == 0), stop=(k == KD - 1))
                                last.then_inc(f_h, 1)
                            for m in range(KE):
                                pe.wait_ge(f_g, r * 4 + (2 * h + m + 1))
                                for c in range(NS):
                                    if m == 0:
                                        pe.wait_ge(f_s, r * 8 + (4 * h - 4 + c + 1) if h else r * 8)
                                    last = pe.matmul(psY[c][:, :], hT[:, h, m, c * P:(c + 1) * P], w2s[:, h, m, :],
                                                     start=(m == 0), stop=(m == KE - 1))
                                    if m == KE - 1:
                                        last.then_inc(f_y, 1)

                @block.scalar
                def _(act):
                    with rounds(act) as r:
                        for h in range(2):
                            for k in range(KD):
                                act.wait_ge(f_xt, r * 8 + (4 * h + k + 1))
                                if k == 0:
                                    act.wait_ge(f_h, r * 4)
                                act.activation(xTb[:, h, k, :], psT[k % 2][:, :], ACT.Copy).then_inc(f_xs, 1)
                            act.wait_ge(f_w[h], r * 64)
                            for m in range(KE):
                                act.wait_ge(f_h, r * 4 + (2 * h + m + 1))
                                if m == 0:
                                    act.wait_ge(f_y, r * 8)
                                act.activation(hT[:, h, m, :], psH[m][:, :], ACT.Gelu, bias=b1s[:, h, m:m + 1]).then_inc(f_g, 1)

                @block.vector
                def _(dve):
                    with rounds(dve) as r:
                        for h in range(2):
                            dve.wait_ge(f_w[h], r * 64)
                            dve.wait_ge(f_hold, r * 6 + (3 * h - 3))
                            for c in range(NS):
                                dve.wait_ge(f_y, r * 8 + (4 * h + c + 1))
                                dve.tensor_tensor(ysum[:, c % 2, :], psY[c][:, :], b2s[:, h, :], ALU.add).then_inc(f_s, 1)
                                dve.wait_ge(f_s, r * 8 + (4 * h + c + 1))
                                dve.tensor_scalar(yout[:, h, c, :], ysum[:, c % 2, :], ids[:, h, c, 1:2].bitcast(F32), None,
                                                  ALU.mult).then_inc(f_o, 1)


_INS = ['x', 'ctx_2048', 'itok_Bx1_68_817', 'g_xattn', 'g_ffn', 'L0_xattn_b', 'L0_ffn_w1', 'L0_ffn_b1',
        'L0_ffn_w2', 'L0_ffn_b2', 'L0_ffn_centroids', 'L0_ffn_w_route']


def kernel(**inputs):
    import numpy as _np
    import concourse.bacc as _bacc
    from concourse import mybir as _mybir
    from concourse.bass_utils import run_bass_kernel_spmd as _run

    nc = _bacc.Bacc("TRN2", target_bir_lowering=False, num_devices=1)
    arrays, args = {}, []
    for name in _INS:
        a = _np.ascontiguousarray(inputs[name])
        arrays[f"in_{name}_dram"] = a
        args.append(nc.dram_tensor(f"in_{name}_dram", a.shape, _mybir.dt.from_np(a.dtype), kind="ExternalInput").ap())
    shape = inputs['x'].shape
    args.append(nc.dram_tensor("out_0_dram", shape, _mybir.dt.float32, kind="ExternalOutput").ap())
    flamingo_kernel(nc, *args)
    r = _run(nc, [arrays], core_ids=[0])
    return r.results[0]["out_0_dram"]
```

```python
from contextlib import ExitStack

import concourse.bass as bass
from concourse import mybir

F32 = mybir.dt.float32
F32R = mybir.dt.float32r
I32 = mybir.dt.int32
ALU = mybir.AluOpType
ACT = mybir.ActivationFunctionType
AX = mybir.AxisListType

P = 128
HG = 4
STEPS_IN_BODY = 8
LN_EPS = 1e-5
NORM_EPS = 1e-12
MASK = -1e12
ROUND = float(3 << 22)
RSQRT_BITS = float(0x5F3759DF)
FAR = float(1 << 20)


class Step:

    def __init__(self, rnd, l, groups):
        self.rnd, self.l, self.groups = rnd, l, groups

    def on(self, off):
        return self.rnd is not None or 0 <= self.l + off < self.groups

    def count(self, per, off, k):
        v = per * (self.l + off) + k
        return v if self.rnd is None else self.rnd * (per * STEPS_IN_BODY) + v

    def batch(self, per, off, k):
        v = per * ((self.l + off) // 4) + k
        return v if self.rnd is None else self.rnd * (per * STEPS_IN_BODY // 4) + v

    def pair(self, per, off, k):
        v = per * ((self.l + off) // 2) + k
        return v if self.rnd is None else self.rnd * (per * STEPS_IN_BODY // 2) + v

    def bpair(self, per, off, k):
        v = per * ((self.l + off) // 8) + k
        return v if self.rnd is None else self.rnd * (per * STEPS_IN_BODY // 8) + v

    def g(self, off=0):
        return (self.l + off) % 4


class Block:

    def __init__(self, rnd, h):
        self.rnd, self.h, self.first = rnd, h, rnd is None

    def front(self, per, off, k):
        return per * off + k if self.first else self.rnd * (2 * per) + (per * (self.h - 1 + off) + k)

    def back(self, per, off, k):
        return self.rnd * (2 * per) + (per * (self.h + off) + k)

    def par(self, off=0):
        return off % 2 if self.first else (1 - self.h + off) % 2

    def pair(self, per, k, off=0):
        return per * (off // 2 + k) if self.first else self.rnd * per + per * ((self.h - 1 + off) // 2 + k)

    def row(self, off):
        return 2 * off if self.first else self.rnd * 4 + 2 * (self.h - 1 + off)


TURNS = [("T0", 3), ("XT", -5), ("T1", 3), ("MT", 1), ("T2", 3), ("RK", -6), ("DT", -1), ("T3", 3), ("OT", -1),
         ("T4", 3), ("LG", -5), ("T5", 3), ("T6", 3), ("T7", 3)]
FIRST, LAST = -8, 7
RSQRT_STEPS = 13


def rsqrt(dve, y, t, v, done, at, first=0, last=RSQRT_STEPS):
    for k in range(first, last):
        if k == 0:
            dve.tensor_scalar(y.bitcast(I32), v.bitcast(I32), -0.5, RSQRT_BITS, ALU.mult, ALU.add).then_inc(done, 1)
            continue
        dve.wait_ge(done, at(k))
        if k % 4 == 1:
            dve.tensor_tensor(t, y, y, ALU.mult).then_inc(done, 1)
        elif k % 4 == 2:
            dve.tensor_tensor(t, t, v, ALU.mult).then_inc(done, 1)
        elif k % 4 == 3:
            dve.tensor_scalar(t, t, -0.5, 1.5, ALU.mult, ALU.add).then_inc(done, 1)
        else:
            dve.tensor_tensor(y, y, t, ALU.mult).then_inc(done, 1)


def turn_table(groups):
    table, k = {}, 0
    for n in range(FIRST, groups + LAST):
        for name, off in TURNS:
            if 0 <= n + off < groups:
                table[(n, name)] = k
                k += 1
    return table


def flamingo_kernel(nc, x, ctx_in, lens, g_xattn, g_ffn, b_in, w1, b1, w2, b2, cent, w_route, out):
    B, S, D = x.shape
    E, _, DE = w1.shape
    H = 16
    DH = D // H
    NG = H // HG
    NT = S // P
    G = B * NG
    TOK = B * S
    KD = D // P
    KE = DE // P
    CAP = TOK
    BLK = 512
    LIST = E * CAP
    EMPTY = 3
    assert NG == 4 and NT == 4 and S == 512 and D == 512 and B % 2 == 0 and E == 8 and DH == 32
    W3 = 3 * DH
    LN1 = RSQRT_STEPS + 10
    LN2 = RSQRT_STEPS + 10
    turns = turn_table(G)
    per_round = len(TURNS) * STEPS_IN_BODY

    x_d = x.rearrange("b (i p) d -> b p i d", p=P)
    c_d = ctx_in.rearrange("b (i p) d -> b p i d", p=P)
    out_d = out.rearrange("b (i p) d -> b p i d", p=P)
    out_rows = out.rearrange("b s d -> (b s) d")
    xn_d = nc.dram_tensor("xn_rows", (TOK, D), F32).ap()
    bm_d = nc.dram_tensor("bias_mask_rows", (B, 2, S), F32).ap()
    list_d = nc.dram_tensor("expert_lists", (LIST + BLK, 2), I32).ap()
    tab_d = nc.dram_tensor("block_table", (P, 2), I32).ap()

    outer = ExitStack()
    with outer:
        def keep(name, shape, dt=F32):
            return outer.enter_context(nc.sbuf_tensor(name, shape, dt))

        def sem(name):
            return outer.enter_context(nc.semaphore(name))

        ident = keep("ident", [P, P])
        ones = keep("ones", [P, P])
        lower = keep("lower", [P, P])
        msum = keep("msum", [P, E])
        tab = keep("tab", [1, 2 * P + 2 * EMPTY + 1], I32)

        hold = keep("hold", [P, 9])

        N_ROUNDS = 2 * (P + EMPTY)

        cnt = keep("cnt", [P, E])
        nblk = keep("nblk", [P, E])
        cum = keep("cum", [P, 2, E])
        qcol_i = keep("qcol_i", [P, 1], I32)
        qcol = keep("qcol", [P, 1])
        earlier = keep("earlier", [P, E])
        scr8 = keep("scr8", [P, E])
        place = keep("place", [P, 6])
        tab_i = keep("tab_i", [P, 2], I32)

        with ExitStack() as ctx:
            def sb(name, shape, dt=F32):
                return ctx.enter_context(nc.sbuf_tensor(name, shape, dt))

            def ps(name, shape):
                return ctx.enter_context(nc.psum_tensor(name, shape, F32))

            stA = sb("stA", [P, 4, HG, S], F32R)
            stB = sb("stB", [P, 4, HG, S], F32R)
            rowQ = sb("rowQ", [P, 2, NT, HG, W3], F32R)
            rowK = sb("rowK", [P, 2, NT, HG, W3], F32R)
            xin = sb("xin", [P, 2, NT, D])
            kin = sb("kin", [P, 2, NT, D])
            vin = sb("vin", [P, 2, NT, D])
            xres = sb("xres", [P, 2, NT, D])
            prob = sb("prob", [P, 2, HG, S])
            xg = sb("xg", [P, 2, NT, P])
            attT = sb("attT", [P, 2, S])
            sumT = sb("sumT", [P, 2, S])
            rsum = sb("rsum", [P, NT, HG])
            scaled = sb("scaled", [P, NT, P])
            xn2 = sb("xn2", [P, 2, D])
            xT = sb("xT", [P, KD, P])
            st6 = sb("st6", [P, NT, 6])
            mv = sb("mv", [P, NT, 2])
            mean = sb("mean", [P, 2, NT])
            varx = sb("varx", [P, NT])
            varx2 = sb("varx2", [P, NT])
            rstd = sb("rstd", [P, 2, NT])
            mx = sb("mx", [P, NT, HG])
            nm = sb("nm", [P, NT, 2, HG], F32R)
            mT = sb("mT", [2 * HG, S], F32R)
            tanh_a = sb("tanh_a", [P, 1])
            tanh_f = sb("tanh_f", [P, 1])
            live = sb("live", [P, B])
            routeT = sb("routeT", [P, KD, 2 * E])
            st6b = sb("st6b", [P, NT, NG, 6])
            mvb = sb("mvb", [P, NT, 2])
            rsb = sb("rsb", [P, 2 * NT])
            rst = sb("rst", [P, 2 * NT])
            varb = sb("varb", [P, 2 * NT])
            nrm = sb("nrm", [P, 3, NT])
            lg = sb("lg", [P, 2 * E])
            logit = sb("logit", [P, E])
            top8 = sb("top8", [P, 8])
            mask = sb("mask", [P, 2, E])
            shifted = sb("shifted", [P, 2, E])
            expo = sb("expo", [P, 2, E])
            chosen = sb("chosen", [P, E])
            gsum = sb("gsum", [P, 1])
            e_off = sb("e_off", [P, E])
            token = sb("token", [P, 1])
            slot_f = sb("slot_f", [P, E])
            slot = sb("slot", [P, 2, E], I32)
            entry = sb("entry", [P, 2, E, 2], I32)
            eo_i = sb("eo_i", [P, E], I32)
            tok_i = sb("tok_i", [P, 1], I32)

            banks = [ps(f"bank{i}", [P, 512]) for i in range(8)]
            psS, psM, psT, psO, psD = banks[0:2], banks[2:4], banks[4:6], banks[6], banks[7]

            with (nc.sbuf_tensor("len_i", [P, B], I32) as len_i,
                  nc.sbuf_tensor("len_f", [P, B], F32) as len_f,
                  nc.sbuf_tensor("len_c", [B, 2], I32) as len_c,
                  nc.sbuf_tensor("len_cf", [B, 2], F32) as len_cf,
                  nc.sbuf_tensor("kpos", [B, S], I32) as kpos,
                  nc.sbuf_tensor("b_split", [B, 2, S], F32R) as b_split,
                  nc.sbuf_tensor("gates_in", [P, 2], F32) as gates_in,
                  nc.sbuf_tensor("cn", [E, 3], F32) as cn,
                  nc.sbuf_tensor("empty", [P, LIST // P, 2], I32) as empty):
                kpos_f = xres[0:B, 0, 0, :]
                b_row = xres[0:B, 0, 1, :]
                b_all = xres[0:B, 0, 2, :]
                cen = xres[0:E, 1, 0, :]
                cen2 = xres[0:E, 1, 1, :]
                wro = xres[0:E, 1, 2, :]
                s_load = sem("setup_loaded")
                s_pool = sem("setup_pool")
                s_dve = sem("setup_dve")
                s_act = sem("setup_act")
                s_pe = sem("setup_pe")
                s_put = sem("setup_stored")
                with nc.Block() as block:
                    @block.sync
                    def _(sp):
                        sp.dma_start(len_i[:, :], lens.rearrange("b a -> a b").to_broadcast([P, B])).then_inc(s_load, 16)
                        sp.dma_start(len_c[:, 0:1], lens).then_inc(s_load, 16)
                        sp.dma_start(b_row, b_in.rearrange("(a s) -> a s", a=1).to_broadcast([B, S])).then_inc(s_load, 16)
                        sp.dma_start(gates_in[:, 0:1], g_xattn.rearrange("(a s) -> a s", a=1).to_broadcast([P, 1])).then_inc(s_load, 16)
                        sp.dma_start(gates_in[:, 1:2], g_ffn.rearrange("(a s) -> a s", a=1).to_broadcast([P, 1])).then_inc(s_load, 16)
                        sp.dma_start(cen, cent).then_inc(s_load, 16)
                        sp.dma_start(wro, w_route).then_inc(s_load, 16)
                        sp.wait_ge(s_pool, 8)
                        sp.dma_start(list_d[0:LIST, :].rearrange("(p c) t -> p c t", p=P), empty[:, :, :]).then_inc(s_put, 16)
                        sp.dma_start(list_d[LIST:LIST + BLK, :].rearrange("(p c) t -> p c t", p=P),
                                     empty[:, 0:BLK // P, :]).then_inc(s_put, 16)
                        sp.wait_ge(s_dve, 12)
                        sp.dma_start(bm_d, b_split[:, :, :].bitcast(F32)).then_inc(s_put, 16)
                        sp.wait_ge(s_put, 48)

                    @block.gpsimd
                    def _(pool):
                        pool.memset(ident[:, :], 0.0).then_inc(s_pool, 1)
                        pool.memset(lower[:, :], 0.0).then_inc(s_pool, 1)
                        pool.memset(ones[:, :], 1.0).then_inc(s_pool, 1)
                        pool.memset(msum[:, :], 0.0).then_inc(s_pool, 1)
                        pool.iota(kpos[:, :], pattern=[[1, S]], base=0, channel_multiplier=0).then_inc(s_pool, 1)
                        pool.iota(eo_i[:, :], pattern=[[CAP, E]], base=-int(FAR), channel_multiplier=0).then_inc(s_pool, 1)
                        pool.iota(tok_i[:, :], pattern=[[0, 1]], base=0, channel_multiplier=1).then_inc(s_pool, 1)
                        pool.memset(empty[:, :, :], int(FAR)).then_inc(s_pool, 1)
                        pool.wait_ge(s_pool, 8)
                        pool.affine_select(out=ident[:, :], in_=ident[:, :], compare_op=ALU.not_equal, fill=1.0,
                                           base=0, pattern=[[-1, P]], channel_multiplier=1).then_inc(s_pool, 1)
                        pool.affine_select(out=lower[:, :], in_=lower[:, :], compare_op=ALU.is_ge, fill=1.0,
                                           base=0, pattern=[[-1, P]], channel_multiplier=1).then_inc(s_pool, 1)

                    @block.vector
                    def _(dve):
                        dve.memset(stA[96:P, :, :, :].bitcast(F32), 1.0)
                        dve.memset(stB[96:P, :, :, :].bitcast(F32), 1.0)
                        dve.wait_ge(s_load, 16 * 7)
                        dve.wait_ge(s_pool, 7)
                        dve.tensor_copy(len_f[:, :], len_i[:, :]).then_inc(s_dve, 1)
                        dve.tensor_copy(len_cf[:, 0:1], len_c[:, 0:1]).then_inc(s_dve, 1)
                        dve.tensor_copy(kpos_f, kpos[:, :]).then_inc(s_dve, 1)
                        dve.wait_ge(s_dve, 3)
                        dve.tensor_scalar(live[:, :], len_f[:, :], 1.0, None, ALU.is_ge).then_inc(s_dve, 1)
                        dve.tensor_scalar(len_cf[:, 1:2], len_cf[:, 0:1], 1.0, None, ALU.is_ge).then_inc(s_dve, 1)
                        dve.tensor_scalar(b_all, kpos_f, len_cf[:, 0:1], MASK, ALU.is_ge, ALU.mult).then_inc(s_dve, 1)
                        dve.tensor_tensor_reduce(cen2, cen, cen, 1.0, 0.0, ALU.mult, ALU.add,
                                                 cn[:, 0:1]).then_inc(s_dve, 1)
                        dve.wait_ge(s_dve, 7)
                        dve.tensor_tensor(kpos_f, b_all, b_row, ALU.add).then_inc(s_dve, 1)
                        dve.tensor_scalar(cn[:, 1:2], cn[:, 0:1], NORM_EPS * NORM_EPS, None, ALU.max).then_inc(s_dve, 1)
                        dve.wait_ge(s_dve, 9)
                        dve.tensor_scalar(b_all, kpos_f, len_cf[:, 1:2], None, ALU.mult).then_inc(s_dve, 1)
                        dve.wait_ge(s_dve, 10)
                        dve.tensor_copy(b_split[:, 0, :], b_all).then_inc(s_dve, 1)
                        dve.wait_ge(s_dve, 11)
                        dve.tensor_tensor(b_split[:, 1, :], b_all, b_split[:, 0, :].bitcast(F32),
                                          ALU.subtract).then_inc(s_dve, 1)
                        dve.tensor_copy(e_off[:, :], eo_i[:, :]).then_inc(s_dve, 1)
                        dve.tensor_copy(token[:, :], tok_i[:, :]).then_inc(s_dve, 1)
                        dve.wait_ge(s_dve, 14)
                        rsqrt(dve, cn[:, 0:1], cn[:, 2:3], cn[:, 1:2], s_dve, lambda k: 14 + k)
                        dve.wait_ge(s_dve, 14 + RSQRT_STEPS)
                        dve.tensor_scalar(cen2, cen, cn[:, 0:1], None, ALU.mult).then_inc(s_dve, 1)
                        dve.wait_ge(s_pe, 1)
                        dve.tensor_copy(routeT[:, :, :], psT[0][:, 0:KD * 2 * E].rearrange("p (k e) -> p k e", k=KD)).then_inc(s_dve, 1)

                    @block.scalar
                    def _(act):
                        act.wait_ge(s_load, 16 * 7)
                        act.activation(tanh_a[:, :], gates_in[:, 0:1], ACT.Tanh).then_inc(s_act, 1)
                        act.activation(tanh_f[:, :], gates_in[:, 1:2], ACT.Tanh).then_inc(s_act, 1)

                    @block.tensor
                    def _(pe):
                        pe.wait_ge(s_load, 16 * 7)
                        pe.wait_ge(s_pool, 10)
                        pe.wait_ge(s_dve, 15 + RSQRT_STEPS)
                        for k in range(KD):
                            pe.transpose(psT[0][:, 2 * E * k:2 * E * k + E], cen2[:, k * P:(k + 1) * P], ident[0:E, 0:E])
                            last = pe.transpose(psT[0][:, 2 * E * k + E:2 * E * k + 2 * E], wro[:, k * P:(k + 1) * P],
                                                ident[0:E, 0:E])
                        last.then_inc(s_pe, 1)

            s_x = [sem(f"x_loaded{i}") for i in range(2)]
            s_k = [sem(f"k_loaded{i}") for i in range(2)]
            s_v = [sem(f"v_loaded{i}") for i in range(2)]
            s_res = [sem(f"residual_loaded{i}") for i in range(2)]
            s_bm = [sem(f"bias_rows_loaded{i}") for i in range(4)]
            s_md = [sem(f"max_rows_placed{i}") for i in range(2)]
            s_x1 = [sem(f"x1_stored{i}") for i in range(2)]
            s_xns = [sem(f"xn2_stored{i}") for i in range(2)]
            s_list = [sem(f"entries_stored{i}") for i in range(2)]
            s_qk = sem("logits_ready")
            s_exp = sem("probs_ready")
            s_pv = sem("pv_done")
            s_out = sem("attention_copied")
            s_rsum = sem("sums_inverted")
            s_x1a = sem("x1_columns")
            s_m = sem("max_logits_ready")
            s_mx = sem("maxima_taken")
            s_nm = sem("neg_max_split")
            s_stat = sem("ln1_stats")
            s_xg = sem("q_normalised")
            s_hi = sem("hi_parts")
            s_lo = sem("lo_parts")
            s_cols = sem("column_statistics")
            s_ln2 = sem("ln2_steps")
            s_xn2 = sem("row_normalised")
            s_route = sem("route_steps")
            s_gexp = sem("gate_exp")
            s_msum = sem("counts_added")
            s_disp = sem("dispatch_steps")
            s_turn = [sem(f"turned{i}") for i in range(2)]
            s_took = [sem(f"turn_taken{i}") for i in range(2)]

            def turn_of(st, name, off=0):
                if st.rnd is None:
                    k = turns[(st.l + off, name)]
                    return k % 2, k // 2
                k = turns[(STEPS_IN_BODY + st.l + off, name)]
                return k % 2, st.rnd * (per_round // 2) + (k // 2 - per_round // 2)

            def put_turn(eng, st, name):
                i, before = turn_of(st, name)
                eng.wait_ge(s_took[i], before)
                return psT[i], s_turn[i]

            def take_turn(eng, st, name):
                i, before = turn_of(st, name)
                eng.wait_ge(s_turn[i], before + 1)
                return psT[i], s_took[i]

            def all_steps(eng, step):
                for n in range(FIRST, 8):
                    step(Step(None, n, G))
                with eng.Fori(1, G // STEPS_IN_BODY - 1) as rnd:
                    for l in range(STEPS_IN_BODY):
                        step(Step(rnd, l, G))
                for n in range(G - STEPS_IN_BODY, G + LAST):
                    step(Step(None, n, G))

            t_pe = sem("table_counts")
            t_dve = sem("table_steps")
            t_pool = sem("table_iota")
            t_sp = sem("table_moved")
            TABLE_STEPS = 22

            block = ctx.enter_context(nc.Block())

            @block.sync
            def _(sp):
                def step(st):
                    if st.g() == 0:
                        par = (st.l // 4) % 2
                        if st.on(8):
                            if st.rnd is not None or st.l >= 0:
                                sp.wait_ge(s_lo, st.count(2, 4, 0))
                            b = st.batch(1, 8, 0)
                            sp.dma_start(xin[:, par, :, :], x_d[bass.ds(b, 1)].rearrange("a p i d -> p (a i) d")).then_inc(s_x[par], 16)
                            sp.dma_start(kin[:, par, :, :], c_d[bass.ds(b, 1), :, :, 0:D].rearrange("a p i d -> p (a i) d")).then_inc(s_k[par], 16)
                        if st.on(0):
                            if st.rnd is not None or st.l >= 8:
                                sp.wait_ge(s_x1[par], st.bpair(16, 0, 0))
                                sp.wait_ge(s_xn2, st.count(1, -4, 0))
                            b = st.batch(1, 0, 0)
                            sp.dma_start(xres[:, par, :, :], x_d[bass.ds(b, 1)].rearrange("a p i d -> p (a i) d")).then_inc(s_res[par], 16)
                    if st.g() == 1 and st.on(4):
                        par = (st.l // 4 + 1) % 2
                        if st.rnd is not None or st.l >= 4:
                            sp.wait_ge(s_pv, st.batch(32, 0, 0))
                        b = st.batch(1, 4, 0)
                        sp.dma_start(vin[:, par, :, :], c_d[bass.ds(b, 1), :, :, D:2 * D].rearrange("a p i d -> p (a i) d")).then_inc(s_v[par], 16)
                    if st.on(3):
                        g = st.g(3)
                        if st.rnd is not None or st.l >= 1:
                            sp.wait_ge(s_qk, st.count(16, 0, 0))
                        b = st.batch(1, 3, 0)
                        for j in range(HG):
                            sp.dma_start(stA[96:98, g, j, :].bitcast(F32), bm_d[bass.ds(b, 1)].rearrange("a t s -> (a t) s")).then_inc(s_bm[g], 16)
                    if st.on(1):
                        i, before = turn_of(st, "MT")
                        sp.wait_ge(s_took[i], before + 1)
                        for t in range(2):
                            sp.dma_start(stB[98 + t:99 + t, st.g(1), :, :].bitcast(F32), mT[HG * t:HG * t + HG, :].bitcast(F32)).then_inc(s_md[(st.l + 1) % 2], 16)
                    if st.g() == 1 and st.on(-5):
                        par = (st.l // 4 + 1) % 2
                        sp.wait_ge(s_x1a, st.batch(4, -4, 4))
                        b = st.batch(1, -4, 0)
                        sp.dma_start(out_d[bass.ds(b, 1)].rearrange("a p i d -> p (a i) d"), xres[:, par, :, :]).then_inc(s_x1[par], 16)
                    if st.on(-4):
                        sp.wait_ge(s_xn2, st.count(1, -4, 1))
                        t = st.count(1, -4, 0)
                        sp.dma_start(xn_d.rearrange("(t p) d -> t p d", p=P)[bass.ds(t, 1)].rearrange("a p d -> (a p) d"),
                                     xn2[:, st.l % 2, :]).then_inc(s_xns[st.l % 2], 16)

                all_steps(sp, step)

                sp.wait_ge(t_dve, TABLE_STEPS)
                sp.dma_start(tab_d, tab_i[:, :]).then_inc(t_sp, 16)
                sp.wait_ge(t_sp, 16)
                sp.dma_start(tab[0:1, 0:2 * P], tab_d.rearrange("(a q) t -> a (q t)", a=1)).then_inc(t_sp, 16)
                sp.wait_ge(t_sp, 32)
                for i in range(2):
                    sp.wait_ge(s_x1[i], 16 * (B // 2))
                    sp.wait_ge(s_xns[i], 16 * (G // 2))

            @block.gpsimd
            def _(pool):
                def step(st):
                    if st.on(4):
                        r = st.l % 2
                        q3 = rowQ[:, r, :, :, :].rearrange("p i h c -> p (i h) c")
                        k3 = rowK[:, r, :, :, :].rearrange("p i h c -> p (i h) c")
                        pool.wait_ge(s_xg, st.count(4, 4, 4))
                        pool.wait_ge(s_hi, st.count(2, 4, 1))
                        pool.tensor_tensor(q3[:, :, 2 * DH:W3], xg[:, r, :, :].rearrange("p i (h c) -> p (i h) c", c=DH),
                                           q3[:, :, 0:DH].bitcast(F32), ALU.subtract).then_inc(s_lo, 1)
                        kpar = ((st.l + 4) // 4) % 2
                        ksrc = kin[:, kpar, :, st.g() * P:(st.g() + 1) * P]
                        pool.wait_ge(s_hi, st.count(2, 4, 2))
                        pool.tensor_tensor(rowK[:, r, :, :, DH:2 * DH], ksrc.rearrange("p i (h c) -> p i h c", c=DH),
                                           rowK[:, r, :, :, 0:DH].bitcast(F32), ALU.subtract).then_inc(s_lo, 1)
                    if st.on(-6):
                        r = st.l % 2
                        pool.wait_ge(s_disp, st.count(7, -6, 7))
                        if st.rnd is not None:
                            pool.tensor_tensor(hold[:, 3 + r:4 + r], ones[:, 0:1], ones[:, 0:1], ALU.add)
                        for e in range(E):
                            pool.indirect_dma_start(list_d, bass.IndirectOffsetOnAxis(ap=slot[:, r, e:e + 1], axis=0),
                                                    entry[:, r, e, :], None, bounds_check=LIST - 1,
                                                    oob_is_err=False).then_inc(s_list[r], 16)

                pool.iota(qcol_i[:, :], pattern=[[0, 1]], base=0, channel_multiplier=1).then_inc(t_pool, 1)
                all_steps(pool, step)
                for i in range(2):
                    pool.wait_ge(s_list[i], 16 * E * (G // 2))

            @block.scalar
            def _(act):
                def evac_stack(st, k):
                    side, j, g = k % 2, k // 2, st.g(3)
                    if k == 0:
                        if st.rnd is not None or st.l >= 1:
                            act.wait_ge(s_qk, st.count(16, 0, 0))
                    bank, took = take_turn(act, st, f"T{k}")
                    dst = (stB, stA)[side]
                    act.activation(dst[0:W3, g, j, :], bank[0:W3, :], ACT.Copy).then_inc(took, 1)

                def step(st):
                    for s in range(16):
                        u, j = s // 4, s % 4
                        if st.on(0):
                            if j == 0 and (u >= 2 or st.rnd is not None or st.l >= 1):
                                act.wait_ge(s_pv, st.count(8, 0, 2 * u - 2))
                            act.wait_ge(s_qk, st.count(16, 0, s + 1))
                            act.activation(prob[:, u % 2, j, :], psS[j % 2][:, :], ACT.Exp).then_inc(s_exp, 1)
                        if j % 2 == 0 and st.on(3):
                            evac_stack(st, 2 * u + j // 2)
                        if s == 1 and st.on(-5):
                            bank, took = take_turn(act, st, "XT")
                            act.activation(xT[:, :, :].rearrange("p k t -> p (k t)"), bank[:, :], ACT.Copy).then_inc(took, 1)
                        if s == 3 and st.on(1):
                            if st.rnd is not None or st.l >= 0:
                                act.wait_ge(s_md[st.l % 2], st.pair(32, 0, 32))
                            bank, took = take_turn(act, st, "MT")
                            act.activation(mT[:, :], bank[0:2 * HG, :], ACT.Copy).then_inc(took, 1)
                        if s in (2, 4) and st.on(-1):
                            name, dst, src, done = ("DT", sumT, psD, 7) if s == 2 else ("OT", attT, psO, 8)
                            act.wait_ge(s_pv, st.count(8, -1, done))
                            if st.rnd is not None or st.l - 1 >= 2:
                                b, before = turn_of(st, name, -2)
                                act.wait_ge(s_turn[b], before + 1)
                            act.activation(dst[:, (st.l + 1) % 2, :], src[:, :], ACT.Copy).then_inc(s_out, 1)
                        if s == 15 and st.on(-5):
                            act.wait_ge(s_route, st.count(4, -5, 4))
                            act.activation(expo[:, (st.l + 1) % 2, :], shifted[:, (st.l + 1) % 2, :], ACT.Exp).then_inc(s_gexp, 1)

                all_steps(act, step)

            @block.tensor
            def _(pe):
                def pv(st, off, u, values):
                    kt = NT - 1 - u
                    g = st.g(off)
                    vpar = ((st.l + off) // 4) % 2
                    if not values:
                        pe.wait_ge(s_exp, st.count(16, off, 4 * u + 4))
                    if u == 0:
                        if values:
                            pe.wait_ge(s_v[vpar], st.bpair(16, off, 16))
                        if st.rnd is not None or st.l + off >= 1:
                            pe.wait_ge(s_out, st.count(2, off, 0 if values else -1))
                    bank = psO if values else psD
                    for j in range(HG):
                        c0 = (HG * g + j) * DH
                        lhs = vin[:, vpar, kt, c0:c0 + DH] if values else ones[:, 0:DH]
                        last = pe.matmul(bank[DH * j:DH * (j + 1), :], lhs, prob[:, u % 2, j, :],
                                         start=(u == 0), stop=(u == NT - 1), skip_group_check=True,
                                         tile_position=(0, DH * j))
                    last.then_inc(s_pv, 1)

                def turn_rows(st, k):
                    side, j = k % 2, k // 2
                    r = (st.l + 3) % 2
                    if k == 0:
                        pe.wait_ge(s_hi, st.count(2, 3, 2))
                        pe.wait_ge(s_lo, st.count(2, 3, 2))
                    bank, done = put_turn(pe, st, f"T{k}")
                    src = (rowQ, rowK)[side]
                    for i in range(NT):
                        last = pe.transpose(bank[0:W3, i * P:(i + 1) * P], src[:, r, i, j, :].bitcast(F32), ident[:, :])
                    last.then_inc(done, 1)

                def step(st):
                    for s in range(16):
                        u, j = s // 4, s % 4
                        if st.on(0):
                            kt, g = NT - 1 - u, st.g()
                            if s == 0:
                                pe.wait_ge(s_md[st.l % 2], st.pair(32, 0, 32))
                            if s >= 2 or st.rnd is not None or st.l >= 1:
                                pe.wait_ge(s_exp, st.count(16, 0, s - 1))
                            pe.matmul(psS[j % 2][:, :], stA[0:100, g, j, kt * P:(kt + 1) * P], stB[0:100, g, j, :],
                                      start=True, stop=True).then_inc(s_qk, 1)
                        if st.on(2):
                            i, g = s // 4, st.g(2)
                            if s == 0:
                                pe.wait_ge(s_bm[g], st.batch(64, 2, 64))
                                for name in ("T6", "T7"):
                                    b, before = turn_of(st, name, -1)
                                    pe.wait_ge(s_took[b], before + 1)
                            if s >= 2 or st.rnd is not None or st.l + 2 >= 1:
                                pe.wait_ge(s_mx, st.count(16, 2, s - 1))
                            pe.matmul(psM[s % 2][:, :], stB[0:98, g, j, i * P:(i + 1) * P], stA[0:98, g, j, :],
                                      start=True, stop=True).then_inc(s_m, 1)
                        if j % 2 == 1:
                            if u > 0 and st.on(0):
                                pv(st, 0, u - 1, j == 3)
                            if u == 0 and st.on(-1):
                                pv(st, -1, NT - 1, j == 3)
                        if j % 2 == 0 and st.on(3):
                            turn_rows(st, 2 * u + j // 2)
                        if s == 1 and st.on(-5):
                            pe.wait_ge(s_xn2, st.count(1, -5, 1))
                            bank, done = put_turn(pe, st, "XT")
                            for k in range(KD):
                                last = pe.transpose(bank[:, k * P:(k + 1) * P], xn2[:, (st.l + 1) % 2, k * P:(k + 1) * P], ident[:, :])
                            last.then_inc(done, 1)
                        if s == 3 and st.on(1):
                            pe.wait_ge(s_nm, st.count(2, 1, 2))
                            bank, done = put_turn(pe, st, "MT")
                            for i in range(NT):
                                last = pe.transpose(bank[0:2 * HG, i * P:(i + 1) * P],
                                                    nm[:, i, :, :].rearrange("p t h -> p (t h)").bitcast(F32), ident[:, :])
                            last.then_inc(done, 1)
                        if s == 5 and st.on(-6):
                            pe.wait_ge(s_route, st.count(4, -6, 4))
                            if st.rnd is not None or st.l >= 7:
                                pe.wait_ge(s_msum, st.count(1, -6, 0))
                            bank, done = put_turn(pe, st, "RK")
                            pe.matmul(bank[:, 0:E], lower[:, :], mask[:, st.l % 2, :], start=True, stop=False)
                            pe.matmul(bank[:, 0:E], ones[:, :], msum[:, :], start=False, stop=True).then_inc(done, 1)
                        if s in (5, 7) and st.on(-1):
                            name, src = ("DT", sumT) if s == 5 else ("OT", attT)
                            pe.wait_ge(s_out, st.count(2, -1, 1 if s == 5 else 2))
                            bank, done = put_turn(pe, st, name)
                            for i in range(NT):
                                last = pe.transpose(bank[:, i * P:(i + 1) * P], src[:, (st.l + 1) % 2, i * P:(i + 1) * P], ident[:, :])
                            last.then_inc(done, 1)
                        if s == 9 and st.on(-5):
                            b, before = turn_of(st, "XT")
                            pe.wait_ge(s_took[b], before + 1)
                            bank, done = put_turn(pe, st, "LG")
                            for k in range(KD):
                                last = pe.matmul(bank[:, 0:2 * E], xT[:, k, :], routeT[:, k, :], start=(k == 0), stop=(k == KD - 1))
                            last.then_inc(done, 1)

                all_steps(pe, step)

                pe.wait_ge(s_mx, 16 * G)
                pe.wait_ge(s_msum, TOK // P)
                pe.matmul(psM[0][:, 0:E], ones[:, :], msum[:, :], start=True, stop=True).then_inc(t_pe, 1)

            @block.vector
            def _(dve):
                def column_stats(st):
                    g, par = st.g(-1), ((st.l - 1) // 4) % 2
                    dve.wait_ge(s_x1a, st.count(1, -1, 1))
                    for i in range(NT):
                        dve.bn_stats(st6b[:, i, g, :], xres[:, par, i, g * P:(g + 1) * P]).then_inc(s_cols, 1)

                def ln2(st, s):
                    c = lambda k: st.batch(LN2, -4, k)
                    if s == 11:
                        dve.wait_ge(s_cols, st.count(4, -1, 4))
                        dve.memset(hold[:, 0:1], 0.0)
                        for i in range(NT):
                            dve.bn_aggr(mvb[:, i, :], st6b[:, i, :, :]).then_inc(s_ln2, 1)
                        dve.wait_ge(s_ln2, c(4))
                        dve.tensor_scalar(varb[:, 0:NT], mvb[:, :, 1], LN_EPS, None, ALU.add).then_inc(s_ln2, 1)
                        dve.tensor_copy(varb[:, NT:2 * NT], mvb[:, :, 1]).then_inc(s_ln2, 1)
                    if s == 12:
                        dve.wait_ge(s_ln2, c(6))
                    if 12 <= s <= 15:
                        rsqrt(dve, rsb[:, :], rst[:, :], varb[:, :], s_ln2, lambda k: c(6 + k),
                              (0, 4, 7, 10)[s - 12], (4, 7, 10, RSQRT_STEPS)[s - 12])
                    if s == 16:
                        dve.wait_ge(s_ln2, c(6 + RSQRT_STEPS))
                        dve.tensor_tensor(nrm[:, 0, :], varb[:, NT:2 * NT], rsb[:, NT:2 * NT], ALU.mult).then_inc(s_ln2, 1)
                        dve.wait_ge(s_ln2, c(LN2 - 3))
                        dve.tensor_tensor(nrm[:, 1, :], nrm[:, 0, :], rsb[:, 0:NT], ALU.mult).then_inc(s_ln2, 1)
                        dve.wait_ge(s_ln2, c(LN2 - 2))
                        dve.tensor_scalar(nrm[:, 1, :], nrm[:, 1, :], float(D) ** 0.5, NORM_EPS, ALU.mult, ALU.max).then_inc(s_ln2, 1)
                        dve.wait_ge(s_ln2, c(LN2 - 1))
                        dve.reciprocal(nrm[:, 2, :], nrm[:, 1, :]).then_inc(s_ln2, 1)

                def normalise(st):
                    i, par = st.g(), ((st.l + 4) // 4) % 2
                    dve.wait_ge(s_ln2, st.batch(LN2, -4, LN2))
                    if st.rnd is not None or st.l - 4 >= 2:
                        dve.wait_ge(s_xns[st.l % 2], st.pair(16, -4, 0))
                    dve.tensor_scalar(xn2[:, st.l % 2, :], xres[:, par, i, :], mvb[:, i, 0:1], rsb[:, i:i + 1],
                                      ALU.subtract, ALU.mult).then_inc(s_xn2, 1)

                def route(st, s):
                    r, i = (st.l + 1) % 2, st.g(-5)
                    c = lambda k: st.count(4, -5, k)
                    if s == 10:
                        bank, took = take_turn(dve, st, "LG")
                        dve.tensor_copy(lg[:, :], bank[:, 0:2 * E]).then_inc(took, 1)
                    if s == 11:
                        dve.wait_ge(s_ln2, st.batch(LN2, -5, LN2))
                        b, before = turn_of(st, "LG")
                        dve.wait_ge(s_took[b], before + 1)
                        dve.scalar_tensor_tensor(out=logit[:, :], in0=lg[:, 0:E], scalar=nrm[:, 2, i:i + 1], in1=lg[:, E:2 * E],
                                                 op0=ALU.mult, op1=ALU.add).then_inc(s_route, 1)
                    if s == 12:
                        dve.wait_ge(s_route, c(1))
                        dve.memset(hold[:, 1:2], 0.0)
                        dve.max(top8[:, :], logit[:, :]).then_inc(s_route, 1)
                    if s == 13:
                        dve.wait_ge(s_route, c(2))
                        dve.tensor_scalar(mask[:, r, :], logit[:, :], top8[:, 1:2], None, ALU.is_ge).then_inc(s_route, 1)
                        dve.tensor_scalar(shifted[:, r, :], logit[:, :], top8[:, 0:1], None, ALU.subtract).then_inc(s_route, 1)

                def dispatch(st, s):
                    r = st.l % 2
                    c = lambda k: st.count(7, -6, k)
                    if s == 5:
                        if st.rnd is not None or st.l - 6 >= 2:
                            dve.wait_ge(s_list[r], st.pair(16 * E, -6, 0))
                        if st.rnd is not None or st.l - 6 >= 1:
                            dve.wait_ge(s_disp, c(0))
                        dve.wait_ge(s_gexp, st.count(1, -6, 1))
                        dve.tensor_tensor_reduce(chosen[:, :], expo[:, r, :], mask[:, r, :], 1.0, 0.0, ALU.mult, ALU.add,
                                                 gsum[:, 0:1]).then_inc(s_disp, 1)
                        bank, took = take_turn(dve, st, "RK")
                        dve.tensor_tensor(slot_f[:, :], bank[:, 0:E], e_off[:, :], ALU.add).then_inc(took, 1)
                    if s == 6:
                        dve.wait_ge(s_disp, c(1))
                        dve.reciprocal(gsum[:, 0:1], gsum[:, 0:1]).then_inc(s_disp, 1)
                        dve.tensor_tensor(msum[:, :], msum[:, :], mask[:, r, :], ALU.add).then_inc(s_msum, 1)
                    if s == 7:
                        b, before = turn_of(st, "RK")
                        dve.wait_ge(s_took[b], before + 1)
                        dve.tensor_tensor(slot_f[:, :], slot_f[:, :], mask[:, r, :], ALU.mult).then_inc(s_disp, 1)
                        dve.wait_ge(s_disp, c(2))
                        dve.tensor_scalar(entry[:, r, :, 1].bitcast(F32), chosen[:, :], gsum[:, 0:1], tanh_f[:, 0:1],
                                          ALU.mult, ALU.mult).then_inc(s_disp, 1)
                    if s == 8:
                        dve.wait_ge(s_disp, c(3))
                        dve.tensor_scalar(slot[:, r, :], slot_f[:, :], FAR, None, ALU.add).then_inc(s_disp, 1)
                        dve.tensor_scalar(entry[:, r, :, 0], mask[:, r, :], 0.0, token[:, 0:1], ALU.mult, ALU.add).then_inc(s_disp, 1)
                        dve.wait_ge(s_disp, c(6))
                        dve.tensor_scalar(token[:, :], token[:, :], float(P), None, ALU.add).then_inc(s_disp, 1)

                def stats(st, i):
                    par = (st.l // 4) % 2
                    if i == 0:
                        dve.wait_ge(s_x[par], st.bpair(16, 8, 16))
                    dve.bn_stats(st6[:, i, :], xin[:, par, i, :]).then_inc(s_stat, 1)
                    dve.wait_ge(s_stat, st.batch(LN1, 8, 2 * i + 1))
                    dve.memset(hold[:, 2:3], 0.0)
                    dve.bn_aggr(mv[:, i, :], st6[:, i, :]).then_inc(s_stat, 1)

                def scale(st, s):
                    par = (st.l // 4) % 2
                    c = lambda k: st.batch(LN1, 8, k)
                    if s == 0:
                        dve.wait_ge(s_stat, c(8))
                        dve.tensor_copy(mean[:, par, :], mv[:, :, 0])
                        dve.tensor_scalar(varx[:, :], mv[:, :, 1], LN_EPS, None, ALU.add).then_inc(s_stat, 1)
                    if s == 1:
                        dve.wait_ge(s_stat, c(9))
                    if 1 <= s <= RSQRT_STEPS:
                        rsqrt(dve, rstd[:, par, :], varx2[:, :], varx[:, :], s_stat, lambda k: c(9 + k), s - 1, s)
                    if s == 14:
                        dve.wait_ge(s_stat, c(9 + RSQRT_STEPS))
                        dve.tensor_scalar(rstd[:, par, :], rstd[:, par, :], live[:, bass.ds(st.batch(1, 8, 0), 1)],
                                          float(DH) ** -0.5, ALU.mult, ALU.mult).then_inc(s_stat, 1)

                def rows(st, part):
                    r, g, par = st.l % 2, st.g(), ((st.l + 4) // 4) % 2
                    if part == 0:
                        dve.wait_ge(s_stat, st.batch(LN1, 4, LN1))
                        if st.rnd is not None or st.l + 4 >= 2:
                            dve.wait_ge(s_lo, st.count(2, 3, 0))
                    if part in (0, 1):
                        for i in range(2 * part, 2 * part + 2):
                            dve.tensor_scalar(xg[:, r, i, :], xin[:, par, i, g * P:(g + 1) * P], mean[:, par, i:i + 1],
                                              rstd[:, par, i:i + 1], ALU.subtract, ALU.mult).then_inc(s_xg, 1)
                    if part == 2:
                        if st.rnd is not None or st.l + 4 >= 2:
                            for name in ("T6", "T7"):
                                b, before = turn_of(st, name, -1)
                                dve.wait_ge(s_turn[b], before + 1)
                        dve.wait_ge(s_xg, st.count(4, 4, 4))
                        dst = rowQ[:, r, :, :, 0:2 * DH].rearrange("p i h (t c) -> p (i h) t c", t=2)
                        src = xg[:, r, :, :].rearrange("p i (h a c) -> p (i h) a c", a=1, c=DH).to_broadcast([P, NT * HG, 2, DH])
                        dve.tensor_copy(dst, src).then_inc(s_hi, 1)
                    if part in (3, 4):
                        t = 2 * (part - 3)
                        if part == 3:
                            dve.wait_ge(s_k[par], st.bpair(16, 4, 16))
                        ins = dve.tensor_copy(rowK[:, r, :, :, t * DH:(t + 1) * DH],
                                              kin[:, par, :, g * P:(g + 1) * P].rearrange("p i (h c) -> p i h c", c=DH))
                        if part == 4:
                            ins.then_inc(s_hi, 1)

                def step(st):
                    for s in range(16):
                        if st.on(2):
                            if s == 0 and (st.rnd is not None or st.l + 2 >= 1):
                                dve.wait_ge(s_nm, st.count(2, 2, 0))
                            dve.wait_ge(s_m, st.count(16, 2, s + 1))
                            dve.tensor_reduce(mx[:, s // 4, s % 4:s % 4 + 1], psM[s % 2][:, :], AX.X, ALU.max).then_inc(s_mx, 1)
                        if s <= 4 and st.on(4):
                            rows(st, s)
                        if 5 <= s <= 8 and st.on(-6):
                            dispatch(st, s)
                        if s == 5 and st.on(-1):
                            bank, took = take_turn(dve, st, "DT")
                            sums = bank[:, :].rearrange("p (i h c) -> p i h c", i=NT, h=HG)[:, :, :, 0]
                            dve.reciprocal(rsum[:, :, :], sums).then_inc(took, 1)
                        if s == 6 and st.on(-1):
                            b, before = turn_of(st, "DT")
                            dve.wait_ge(s_took[b], before + 1)
                            dve.tensor_scalar(rsum[:, :, :], rsum[:, :, :], tanh_a[:, 0:1], None, ALU.mult).then_inc(s_rsum, 1)
                        if s == 7 and st.on(-1):
                            dve.wait_ge(s_rsum, st.count(1, -1, 1))
                            bank, took = take_turn(dve, st, "OT")
                            each = rsum[:, :, :].rearrange("p i (h a) -> p (i h) a", a=1).to_broadcast([P, NT * HG, DH])
                            dve.tensor_tensor(scaled[:, :, :].rearrange("p i (h c) -> p (i h) c", h=HG),
                                              bank[:, :].rearrange("p (h c) -> p h c", c=DH), each, ALU.mult).then_inc(took, 1)
                        if s == 8 and st.on(-1):
                            g, par = st.g(-1), ((st.l - 1) // 4) % 2
                            if g == 0:
                                dve.wait_ge(s_res[par], st.bpair(16, -1, 16))
                            b, before = turn_of(st, "OT")
                            dve.wait_ge(s_took[b], before + 1)
                            dst = xres[:, par, :, g * P:(g + 1) * P]
                            dve.tensor_tensor(dst, dst, scaled[:, :, :], ALU.add).then_inc(s_x1a, 1)
                        if 10 <= s <= 13 and st.on(-5):
                            route(st, s)
                        if s == 9 and st.on(-1):
                            column_stats(st)
                        if s >= 11 and st.g() == 0 and st.on(-4):
                            ln2(st, s)
                        if st.g() in (1, 2) and s in (6, 11) and st.on(8 - st.g()):
                            stats(st, 2 * (st.g() - 1) + s // 11)
                        if st.g() == 3 and s <= 14 and st.on(5):
                            scale(st, s)
                    if st.on(-4):
                        if st.g() == 0:
                            ln2(st, 16)
                        normalise(st)
                    if st.on(2):
                        dve.wait_ge(s_mx, st.count(16, 2, 16))
                        if st.rnd is not None or st.l + 2 >= 1:
                            b, before = turn_of(st, "MT")
                            dve.wait_ge(s_turn[b], before + 1)
                        dve.tensor_scalar(nm[:, :, 0, :], mx[:, :, :], -1.0, None, ALU.mult).then_inc(s_nm, 1)
                        dve.wait_ge(s_nm, st.count(2, 2, 1))
                        dve.scalar_tensor_tensor(out=nm[:, :, 1, :], in0=mx[:, :, :], scalar=-1.0,
                                                 in1=nm[:, :, 0, :].bitcast(F32), op0=ALU.mult, op1=ALU.subtract).then_inc(s_nm, 1)

                all_steps(dve, step)

                done = 0

                def then(ins):
                    nonlocal done
                    done += 1
                    ins.then_inc(t_dve, 1)
                    dve.wait_ge(t_dve, done)

                for t in range(EMPTY):
                    dve.memset(tab[0:1, 2 * (P + t):2 * (P + t) + 1], LIST)
                    dve.memset(tab[0:1, 2 * (P + t) + 1:2 * (P + t) + 2], E - 1)
                dve.wait_ge(t_pe, 1)
                dve.wait_ge(t_pool, 1)
                then(dve.tensor_copy(qcol[:, :], qcol_i[:, :]))
                then(dve.tensor_scalar(cnt[:, :], psM[0][:, 0:E], (BLK - 1) / 2.0, 1.0 / BLK, ALU.add, ALU.mult))
                then(dve.tensor_scalar(cnt[:, :], cnt[:, :], ROUND, None, ALU.add))
                then(dve.tensor_scalar(nblk[:, :], cnt[:, :], ROUND, None, ALU.subtract))
                then(dve.tensor_copy(cum[:, 0, :], nblk[:, :]))
                src = 0
                for k in (1, 2, 4):
                    then(dve.tensor_copy(cum[:, 1 - src, 0:k], cum[:, src, 0:k]))
                    then(dve.tensor_tensor(cum[:, 1 - src, k:E], cum[:, src, k:E], cum[:, src, 0:E - k], ALU.add))
                    src = 1 - src
                then(dve.tensor_scalar(earlier[:, :], cum[:, src, :], qcol[:, 0:1], None, ALU.is_le))
                then(dve.tensor_reduce(place[:, 0:1], earlier[:, :], AX.X, ALU.add))
                then(dve.tensor_tensor_reduce(scr8[:, :], earlier[:, :], nblk[:, :], 1.0, 0.0, ALU.mult, ALU.add,
                                              place[:, 1:2]))
                then(dve.tensor_tensor(place[:, 2:3], qcol[:, :], place[:, 1:2], ALU.subtract))
                then(dve.tensor_scalar(place[:, 2:3], place[:, 2:3], float(BLK), None, ALU.mult))
                then(dve.tensor_scalar(place[:, 3:4], place[:, 0:1], float(CAP), place[:, 2:3], ALU.mult, ALU.add))
                then(dve.tensor_scalar(tab_i[:, 0:1], place[:, 3:4], float(LIST), None, ALU.min))
                then(dve.tensor_scalar(tab_i[:, 1:2], place[:, 0:1], float(E - 1), None, ALU.min))
                then(dve.tensor_scalar(place[:, 4:5], cum[:, src, E - 1:E], 0.5, 0.25, ALU.mult, ALU.add))
                then(dve.tensor_scalar(place[:, 5:6], place[:, 4:5], ROUND, None, ALU.add))
                then(dve.tensor_scalar(tab[0:1, N_ROUNDS:N_ROUNDS + 1], place[0:1, 5:6], ROUND, None, ALU.subtract))
                assert done == TABLE_STEPS

        with ExitStack() as ctx:
            def sb(name, shape, dt=F32):
                return ctx.enter_context(nc.sbuf_tensor(name, shape, dt))

            def ps(name, shape):
                return ctx.enter_context(nc.psum_tensor(name, shape, F32))

            NS = BLK // P
            w1s = sb("w1s", [P, KD, DE])
            w2s = sb("w2s", [P, KE, D])
            w1p = sb("w1_parts", [P, 2, KD, DE], F32R)
            w2p = sb("w2_parts", [P, 2, KE, D], F32R)
            b1s = sb("b1s", [P, 2, KE])
            b2s = sb("b2s", [P, 2, D])
            gids = sb("gather_ids", [P, 2, NS, 2], I32)
            ids = sb("entries", [P, 2, NS, 2], I32)
            rows = sb("rows_in", [P, 2, NS, D])
            xTb = sb("turned_parts", [P, 2, KD, BLK], F32R)
            gelu = sb("gelu", [P, KE, BLK])
            hT = sb("gelu_parts", [P, 2, KE, BLK], F32R)
            ysum = sb("out_gated_rows", [P, NS, D])
            yout = sb("yout", [P, 2, NS, D])
            banks = [ps(f"bankb{i}", [P, 512]) for i in range(8)]
            psT, psH, psY = banks[0:2], banks[2:4], banks[4:8]
            f_gid = [sem(f"gather_ids_loaded{i}") for i in range(2)]
            f_sid = [sem(f"entries_loaded{i}") for i in range(2)]
            f_b1 = [sem(f"bias1_loaded{i}") for i in range(2)]
            f_b2 = [sem(f"bias2_loaded{i}") for i in range(2)]
            f_w1, f_w2 = sem("weights1_loaded"), sem("weights2_loaded")
            f_rows = [sem(f"rows_gathered{i}") for i in range(2)]
            f_add = [sem(f"rows_added{i}") for i in range(2)]
            f_whi = sem("weights_hi")
            f_wlo = sem("weights_lo")
            f_xt = sem("rows_turned")
            f_xhi = sem("turned_hi")
            f_xlo = sem("turned_lo")
            f_h = sem("hidden_ready")
            f_g = sem("gelu_done")
            f_hs = sem("gelu_split")
            f_y = sem("out_ready")
            f_yg = sem("out_gated")
            f_yo = sem("out_done")
            f_hold = sem("pool_held")
            f_clear = sem("rows_cleared")

            adds = [(f_y, 2 * NS), (f_yg, 2 * NS), (f_yo, 2 * NS), (f_hold, 5)]
            with nc.Block() as block:
                @block.sync
                def _(sp):
                    for start_of, count in adds:
                        sp.sem_inc(start_of, count)

            def n_rounds(eng):
                return eng.value_load(tab[0:1, N_ROUNDS:N_ROUNDS + 1], min_val=1, max_val=P // 2)

            def rounds(eng, step):
                step(Block(None, 0))
                with eng.Fori(1, n_rounds(eng) + 1) as r:
                    for h in range(2):
                        step(Block(r, h))

            def split_product(pe, bank, wts, mov, start, stop):
                for i, (p, q) in enumerate(((0, 0), (0, 1), (1, 0))):
                    last = pe.matmul(bank, wts(p), mov(q), start=start and i == 0, stop=stop and i == 2)
                return last

            with nc.Block() as block:
                @block.sync
                def _(sp):
                    def start_of(at):
                        return sp.value_load(tab[0:1, bass.ds(at, 1)], min_val=0, max_val=LIST)

                    def expert_of(at):
                        return sp.value_load(tab[0:1, bass.ds(at + 1, 1)], min_val=0, max_val=E - 1)

                    def load_gather_ids(start, par):
                        sp.dma_start(gids[:, par, :, :], list_d[bass.ds(start, BLK), :].rearrange("(c p) t -> p c t", p=P)).then_inc(f_gid[par], 16)

                    def load_entries(start, par):
                        sp.dma_start(ids[:, par, :, :], list_d[bass.ds(start, BLK), :].rearrange("(c p) t -> p c t", p=P)).then_inc(f_sid[par], 16)

                    def load_b1(expert, par):
                        sp.dma_start(b1s[:, par, :], b1[bass.ds(expert, 1)].rearrange("a (k p) -> p (a k)", p=P),
                                     allow_slow_non_contiguous=True).then_inc(f_b1[par], 16)

                    def load_b2(expert, par):
                        sp.dma_start(b2s[:, par, :], b2[bass.ds(expert, 1), :].to_broadcast([P, D])).then_inc(f_b2[par], 16)

                    def load_w1(expert):
                        sp.dma_start(w1s[:, :, :], w1[bass.ds(expert, 1)].rearrange("a (k p) n -> p (a k) n", p=P)).then_inc(f_w1, 16)

                    def load_w2(expert):
                        sp.dma_start(w2s[:, :, :], w2[bass.ds(expert, 1)].rearrange("a (k p) n -> p (a k) n", p=P)).then_inc(f_w2, 16)

                    start, expert = start_of(0), expert_of(0)
                    load_gather_ids(start, 0)
                    load_gather_ids(start_of(2), 1)
                    load_w1(expert)
                    load_w2(expert)
                    load_b1(expert, 0)
                    load_entries(start, 0)
                    load_b2(expert, 0)
                    load_b2(expert_of(2), 1)

                    def step(st):
                        start, start_next = start_of(st.row(0)), start_of(st.row(2))
                        expert_next = expert_of(st.row(1))
                        sp.wait_ge(f_rows[st.par()], st.pair(16 * NS, 1))
                        load_gather_ids(start_next, st.par())
                        if not st.first:
                            sp.wait_ge(f_g, st.front(KE, -1, KE))
                        load_b1(expert_next, st.par(1))
                        sp.wait_ge(f_wlo, st.front(2, 0, 1))
                        load_w1(expert_next)
                        if not st.first:
                            sp.wait_ge(f_yo, st.back(NS, 0, NS))
                            load_b2(expert_next, st.par(1))
                        sp.wait_ge(f_wlo, st.front(2, 0, 2))
                        load_w2(expert_next)
                        if not st.first:
                            sp.wait_ge(f_hold, st.rnd * 5 + 4 * st.h)
                            load_entries(start, st.par())

                    rounds(sp, step)

                @block.gpsimd
                def _(pool):
                    def carry_wait():
                        pool.tensor_tensor(hold[:, 5:6], ones[:, 0:1], ones[:, 0:1], ALU.add).then_inc(f_hold, 1)

                    def gather(par):
                        for c in range(NS):
                            pool.indirect_dma_start(rows[:, par, c, :], None, xn_d,
                                                    bass.IndirectOffsetOnAxis(ap=gids[:, par, c, 0:1], axis=0),
                                                    bounds_check=TOK - 1, oob_is_err=False).then_inc(f_rows[par], 16)

                    def step(st):
                        if st.first:
                            for i in range(2):
                                pool.wait_ge(f_clear, i + 1)
                                pool.wait_ge(f_gid[i], 16)
                                gather(i)
                            return
                        h = st.h
                        pool.wait_ge(f_hold, st.rnd * 5 + 2 * h)
                        pool.wait_ge(f_gid[st.par(1)], st.pair(16, 1, 1))
                        pool.wait_ge(f_xt, st.front(KD, -1, KD))
                        carry_wait()
                        gather(st.par(1))
                        pool.wait_ge(f_hold, st.rnd * 5 + 2 * h + 1)
                        if h == 1:
                            pool.wait_ge(f_add[0], st.rnd * (16 * NS))
                        pool.wait_ge(f_yo, st.back(NS, 0, NS))
                        carry_wait()
                        for c in range(NS):
                            pool.indirect_dma_start(out_rows, bass.IndirectOffsetOnAxis(ap=ids[:, h, c, 0:1], axis=0),
                                                    yout[:, h, c, :], None, bounds_check=TOK - 1, oob_is_err=False,
                                                    compute_op=ALU.add).then_inc(f_add[h], 16)
                        if h == 1:
                            pool.wait_ge(f_hold, st.rnd * 5 + 4)
                            pool.wait_ge(f_add[1], st.rnd * (16 * NS))
                            carry_wait()

                    rounds(pool, step)
                    n = n_rounds(pool)
                    for i in range(2):
                        pool.wait_ge(f_gid[i], n * 16 + (32 - 16 * i))
                        pool.wait_ge(f_sid[i], n * 16 + (16 - 16 * i))
                        pool.wait_ge(f_b1[i], n * 16 + 16)
                        pool.wait_ge(f_b2[i], n * 16 + 16)
                        pool.wait_ge(f_rows[i], n * (16 * NS) + 16 * NS)
                    pool.wait_ge(f_w1, n * 32 + 32)
                    pool.wait_ge(f_w2, n * 32 + 32)

                @block.tensor
                def _(pe):
                    def turn(st, k):
                        if k >= 2 or not st.first:
                            pe.wait_ge(f_xlo, st.front(KD, 0, k - 1))
                        for c in range(NS):
                            last = pe.transpose(psT[k % 2][:, c * P:(c + 1) * P], rows[:, st.par(), c, k * P:(k + 1) * P], ident[:, :])
                        last.then_inc(f_xt, 1)

                    def second(st, m):
                        pe.wait_ge(f_hs, st.front(2 * KE, -1, 2 * m + 2))
                        if m == 0:
                            pe.wait_ge(f_wlo, st.front(2, -1, 2))
                        for c in range(NS):
                            if m == 0:
                                pe.wait_ge(f_yg, st.back(NS, -1, c + 1))
                            last = split_product(pe, psY[c][:, :], lambda p: hT[:, p, m, c * P:(c + 1) * P],
                                                 lambda p: w2p[:, p, m, :], m == 0, m == KE - 1)
                            if m == KE - 1:
                                last.then_inc(f_y, 1)

                    def step(st):
                        pe.wait_ge(f_rows[st.par()], st.pair(16 * NS, 1))
                        turn(st, 0)
                        turn(st, 1)
                        if not st.first:
                            second(st, 0)
                        turn(st, 2)
                        turn(st, 3)
                        if not st.first:
                            second(st, 1)
                        pe.wait_ge(f_wlo, st.front(2, 0, 1))
                        for m in range(KE):
                            if not st.first:
                                pe.wait_ge(f_g, st.front(KE, -1, m + 1))
                            for k in range(KD):
                                if m == 0:
                                    pe.wait_ge(f_xlo, st.front(KD, 0, k + 1))
                                last = split_product(pe, psH[m][:, :], lambda p: w1p[:, p, k, m * P:(m + 1) * P],
                                                     lambda p: xTb[:, p, k, :], k == 0, k == KD - 1)
                            last.then_inc(f_h, 1)

                    rounds(pe, step)

                @block.scalar
                def _(act):
                    def take_turned(st, k):
                        act.wait_ge(f_xt, st.front(KD, 0, k + 1))
                        if k == 0 and not st.first:
                            act.wait_ge(f_h, st.front(KE, 0, 0))
                        act.activation(xTb[:, 0, k, :], psT[k % 2][:, :], ACT.Copy).then_inc(f_xhi, 1)

                    def step(st):
                        take_turned(st, 0)
                        take_turned(st, 1)
                        act.wait_ge(f_w1, st.front(16, 0, 16))
                        act.activation(w1p[:, 0, :, :], w1s[:, :, :], ACT.Copy).then_inc(f_whi, 1)
                        take_turned(st, 2)
                        take_turned(st, 3)
                        if not st.first:
                            act.wait_ge(f_sid[st.h], st.rnd * 16)
                            for c in range(NS):
                                act.wait_ge(f_y, st.back(NS, 0, c + 1))
                                act.wait_ge(f_yo, st.back(NS, -1, c + 1))
                                act.activation(ysum[:, c, :], psY[c][:, :], ACT.Copy, scale=ids[:, st.h, c, 1:2].bitcast(F32)).then_inc(f_yg, 1)
                        act.wait_ge(f_w2, st.front(16, 0, 16))
                        act.activation(w2p[:, 0, :, :], w2s[:, :, :], ACT.Copy).then_inc(f_whi, 1)
                        act.wait_ge(f_b1[st.par()], st.pair(16, 1))
                        for m in range(KE):
                            act.wait_ge(f_h, st.front(KE, 0, m + 1))
                            if not st.first:
                                act.wait_ge(f_hs, st.front(2 * KE, -1, 2 * m + 2))
                            act.activation(gelu[:, m, :], psH[m][:, :], ACT.Gelu, bias=b1s[:, st.par(), m:m + 1]).then_inc(f_g, 1)

                    rounds(act, step)

                @block.vector
                def _(dve):
                    def take_turned(st, k):
                        dve.wait_ge(f_xhi, st.front(KD, 0, k + 1))
                        dve.tensor_tensor(xTb[:, 1, k, :], psT[k % 2][:, :], xTb[:, 0, k, :].bitcast(F32), ALU.subtract).then_inc(f_xlo, 1)

                    def step(st):
                        take_turned(st, 0)
                        take_turned(st, 1)
                        dve.wait_ge(f_whi, st.front(2, 0, 1))
                        dve.tensor_tensor(w1p[:, 1, :, :], w1s[:, :, :], w1p[:, 0, :, :].bitcast(F32), ALU.subtract).then_inc(f_wlo, 1)
                        take_turned(st, 2)
                        take_turned(st, 3)
                        if not st.first:
                            dve.wait_ge(f_b2[st.h], st.rnd * 16)
                            dve.wait_ge(f_hold, st.rnd * 5 - 1 + st.h)
                            for c in range(NS):
                                dve.wait_ge(f_yg, st.back(NS, 0, c + 1))
                                dve.scalar_tensor_tensor(out=yout[:, st.h, c, :], in0=b2s[:, st.h, :], scalar=ids[:, st.h, c, 1:2].bitcast(F32),
                                                         in1=ysum[:, c, :], op0=ALU.mult, op1=ALU.add).then_inc(f_yo, 1)
                        dve.wait_ge(f_whi, st.front(2, 0, 2))
                        dve.tensor_tensor(w2p[:, 1, :, :], w2s[:, :, :], w2p[:, 0, :, :].bitcast(F32), ALU.subtract).then_inc(f_wlo, 1)
                        for m in range(KE):
                            dve.wait_ge(f_g, st.front(KE, 0, m + 1))
                            dve.tensor_copy(hT[:, 0, m, :], gelu[:, m, :]).then_inc(f_hs, 1)
                            dve.wait_ge(f_hs, st.front(2 * KE, 0, 2 * m + 1))
                            dve.tensor_tensor(hT[:, 1, m, :], gelu[:, m, :], hT[:, 0, m, :].bitcast(F32), ALU.subtract).then_inc(f_hs, 1)

                    for i in range(2):
                        dve.memset(rows[:, i, :, :], 0.0).then_inc(f_clear, 1)
                    rounds(dve, step)


_INS = ['x', 'ctx_2048', 'itok_Bx1_68_817', 'g_xattn', 'g_ffn', 'L0_xattn_b', 'L0_ffn_w1', 'L0_ffn_b1',
        'L0_ffn_w2', 'L0_ffn_b2', 'L0_ffn_centroids', 'L0_ffn_w_route']


def kernel(**inputs):
    import numpy as _np
    import concourse.bacc as _bacc
    from concourse import mybir as _mybir
    from concourse.bass_utils import run_bass_kernel_spmd as _run

    nc = _bacc.Bacc("TRN2", target_bir_lowering=False, num_devices=1)
    arrays, args = {}, []
    for name in _INS:
        a = _np.ascontiguousarray(inputs[name])
        arrays[f"in_{name}_dram"] = a
        args.append(nc.dram_tensor(f"in_{name}_dram", a.shape, _mybir.dt.from_np(a.dtype), kind="ExternalInput").ap())
    shape = inputs['x'].shape
    args.append(nc.dram_tensor("out_0_dram", shape, _mybir.dt.float32, kind="ExternalOutput").ap())
    flamingo_kernel(nc, *args)
    r = _run(nc, [arrays], core_ids=[0])
    return r.results[0]["out_0_dram"]
```
